# Optimizing a Trainium2 kernel written in Bass

```python
import numpy as np
import jax
import jax.numpy as jnp

def _softmax(x, axis=-1):
    return jax.nn.softmax(x, axis=axis)

def _gelu(x):
    return jax.nn.gelu(x, approximate=True)

def _silu(x):
    return jax.nn.silu(x)

def _sigmoid(x):
    return jax.nn.sigmoid(x)

def _layernorm(x, axis=-1, eps=1e-05):
    m = jnp.mean(x, axis=axis, keepdims=True)
    v = jnp.var(x, axis=axis, keepdims=True)
    return (x - m) / jnp.sqrt(v + eps)

def _scatter_add(tgt, idx, src, axis=0):
    return tgt.at[idx].add(src)

def _segment_sum(src, seg, n):
    return jax.ops.segment_sum(src, seg, n)
kernel_name = 'mk_prb_d1_jaxref_r8_159442'

def setup_inputs(seed: int=0):
    np.random.seed(seed)
    _w = jnp.asarray

    def _L0_attn_setup():
        import jax, jax.numpy as jnp
        import numpy as np
        B, S, D, Hd = (4, 512, 128, 128)

        def _linear_scan(a, x, reverse):

            def comb(l, r):
                al, bl = l
                ar, br = r
                return (al * ar, bl * ar + br)
            _, h = jax.lax.associative_scan(comb, (a, x), axis=1, reverse=reverse)
            return h

        def _rglru(x, a_logit, Wx, bx, Wgx, bgx, Wga, bga, Wo, bo, reverse):
            a_expit = jax.nn.sigmoid(a_logit)
            x = x @ Wx + bx
            gate_x = jax.nn.sigmoid(x @ Wgx + bgx)
            gate_a = jax.nn.sigmoid(x @ Wga + bga)
            a = gate_a * a_expit
            xin = jnp.sqrt(1.0 - a * a) * (gate_x * x)
            h = _linear_scan(a, xin, reverse)
            return h @ Wo + bo
        key = jax.random.key(seed)
        ks = jax.random.split(key, 24)
        f32 = jnp.float32

        def w(k, fan_in, shape):
            return (jax.random.normal(k, shape) / np.sqrt(fan_in)).astype(f32)

        def a_init(k):
            u = jax.random.uniform(k, (Hd,), minval=0.9, maxval=0.999)
            return (jnp.log(u) - jnp.log1p(-u)).astype(f32)
        inp = {'x': jax.random.normal(ks[0], (B, S, D), dtype=f32)}
        for i, pfx in enumerate(['fwd', 'bwd']):
            o = 1 + i * 10
            inp[f'{pfx}_a_logit'] = a_init(ks[o])
            inp[f'{pfx}_Wx'] = w(ks[o + 1], D, (D, Hd))
            inp[f'{pfx}_bx'] = jnp.zeros((Hd,), f32)
            inp[f'{pfx}_Wgx'] = w(ks[o + 2], Hd, (Hd, Hd))
            inp[f'{pfx}_bgx'] = jnp.zeros((Hd,), f32)
            inp[f'{pfx}_Wga'] = w(ks[o + 3], Hd, (Hd, Hd))
            inp[f'{pfx}_bga'] = jnp.zeros((Hd,), f32)
            inp[f'{pfx}_Wo'] = w(ks[o + 4], Hd, (Hd, D))
            inp[f'{pfx}_bo'] = jnp.zeros((D,), f32)
        inp['ld_W'] = w(ks[22], D, (D, D))
        inp['ld_b'] = jnp.zeros((D,), f32)
        return inp
    _L0_attn_in = _L0_attn_setup()

    def _L0_ffn_setup():
        import jax, jax.numpy as jnp
        import numpy as np
        D_MODEL = 128
        D_FF = 256
        NUM_EXPERTS = 16
        TOP_K = 2
        CAPACITY_FACTOR = 1.25
        BATCH, SEQ = (4, 256)
        key = jax.random.key(seed)
        k0, k1, k2, k3 = jax.random.split(key, 4)
        x = jax.random.normal(k0, (BATCH, SEQ, D_MODEL), jnp.float32)
        gate_w = jax.random.normal(k1, (NUM_EXPERTS, D_MODEL), jnp.float32) / np.float32(np.sqrt(D_MODEL))
        w1 = jax.random.normal(k2, (NUM_EXPERTS, D_MODEL, D_FF), jnp.float32) / np.float32(np.sqrt(D_MODEL))
        w2 = jax.random.normal(k3, (NUM_EXPERTS, D_FF, D_MODEL), jnp.float32) / np.float32(np.sqrt(D_FF))
        return {'x': x, 'gate_w': gate_w, 'w1': w1, 'w2': w2}
    _L0_ffn_in = _L0_ffn_setup()
    _d = {'L0_attn_x': _L0_attn_in['x'], 'L0_attn_fwd_a_logit': _L0_attn_in['fwd_a_logit'], 'L0_attn_fwd_Wx': _L0_attn_in['fwd_Wx'], 'L0_attn_fwd_bx': _L0_attn_in['fwd_bx'], 'L0_attn_fwd_Wgx': _L0_attn_in['fwd_Wgx'], 'L0_attn_fwd_bgx': _L0_attn_in['fwd_bgx'], 'L0_attn_fwd_Wga': _L0_attn_in['fwd_Wga'], 'L0_attn_fwd_bga': _L0_attn_in['fwd_bga'], 'L0_attn_fwd_Wo': _L0_attn_in['fwd_Wo'], 'L0_attn_fwd_bo': _L0_attn_in['fwd_bo'], 'L0_attn_bwd_a_logit': _L0_attn_in['bwd_a_logit'], 'L0_attn_bwd_Wx': _L0_attn_in['bwd_Wx'], 'L0_attn_bwd_bx': _L0_attn_in['bwd_bx'], 'L0_attn_bwd_Wgx': _L0_attn_in['bwd_Wgx'], 'L0_attn_bwd_bgx': _L0_attn_in['bwd_bgx'], 'L0_attn_bwd_Wga': _L0_attn_in['bwd_Wga'], 'L0_attn_bwd_bga': _L0_attn_in['bwd_bga'], 'L0_attn_bwd_Wo': _L0_attn_in['bwd_Wo'], 'L0_attn_bwd_bo': _L0_attn_in['bwd_bo'], 'L0_attn_ld_W': _L0_attn_in['ld_W'], 'L0_attn_ld_b': _L0_attn_in['ld_b'], 'L0_ffn_gate_w': _L0_ffn_in['gate_w'], 'L0_ffn_w1': _L0_ffn_in['w1'], 'L0_ffn_w2': _L0_ffn_in['w2']}
    _x0 = _d['L0_attn_x']
    _d['L0_attn_x'] = jax.random.normal(jax.random.fold_in(jax.random.key(seed), 1), (8, 256, 128), dtype=_x0.dtype)
    del _x0
    return _d

def reference(L0_attn_x, L0_attn_fwd_a_logit, L0_attn_fwd_Wx, L0_attn_fwd_bx, L0_attn_fwd_Wgx, L0_attn_fwd_bgx, L0_attn_fwd_Wga, L0_attn_fwd_bga, L0_attn_fwd_Wo, L0_attn_fwd_bo, L0_attn_bwd_a_logit, L0_attn_bwd_Wx, L0_attn_bwd_bx, L0_attn_bwd_Wgx, L0_attn_bwd_bgx, L0_attn_bwd_Wga, L0_attn_bwd_bga, L0_attn_bwd_Wo, L0_attn_bwd_bo, L0_attn_ld_W, L0_attn_ld_b, L0_ffn_gate_w, L0_ffn_w1, L0_ffn_w2):

    def _L0_attn_ref(x, fwd_a_logit, fwd_Wx, fwd_bx, fwd_Wgx, fwd_bgx, fwd_Wga, fwd_bga, fwd_Wo, fwd_bo, bwd_a_logit, bwd_Wx, bwd_bx, bwd_Wgx, bwd_bgx, bwd_Wga, bwd_bga, bwd_Wo, bwd_bo, ld_W, ld_b):
        import jax, jax.numpy as jnp
        import numpy as np
        B, S, D, Hd = (4, 512, 128, 128)

        def _linear_scan(a, x, reverse):

            def comb(l, r):
                al, bl = l
                ar, br = r
                return (al * ar, bl * ar + br)
            _, h = jax.lax.associative_scan(comb, (a, x), axis=1, reverse=reverse)
            return h

        def _rglru(x, a_logit, Wx, bx, Wgx, bgx, Wga, bga, Wo, bo, reverse):
            a_expit = jax.nn.sigmoid(a_logit)
            x = x @ Wx + bx
            gate_x = jax.nn.sigmoid(x @ Wgx + bgx)
            gate_a = jax.nn.sigmoid(x @ Wga + bga)
            a = gate_a * a_expit
            xin = jnp.sqrt(1.0 - a * a) * (gate_x * x)
            h = _linear_scan(a, xin, reverse)
            return h @ Wo + bo
        last_scale = 1.0
        identity = x
        xg = jax.nn.gelu(x)
        x_fwd = _rglru(xg, fwd_a_logit, fwd_Wx, fwd_bx, fwd_Wgx, fwd_bgx, fwd_Wga, fwd_bga, fwd_Wo, fwd_bo, reverse=False)
        x_bwd = _rglru(xg, bwd_a_logit, bwd_Wx, bwd_bx, bwd_Wgx, bwd_bgx, bwd_Wga, bwd_bga, bwd_Wo, bwd_bo, reverse=True)
        x = (x_fwd + x_bwd) / 2 + identity
        x = jax.nn.gelu(x) @ ld_W + ld_b + identity
        return last_scale * x

    def _L0_ffn_ref(x, gate_w, w1, w2):
        import jax, jax.numpy as jnp
        import numpy as np
        D_MODEL = 128
        D_FF = 256
        NUM_EXPERTS = 16
        TOP_K = 2
        CAPACITY_FACTOR = 1.25
        BATCH, SEQ = (4, 256)
        B, S, d = x.shape
        T = B * S
        E, K = (NUM_EXPERTS, TOP_K)
        capacity = int(CAPACITY_FACTOR * T * K / E)
        xf = x.reshape(T, d)
        logits = xf @ gate_w.T
        probs = jax.nn.sigmoid(logits)
        top_vals, sel = jax.lax.top_k(probs, K)
        weights = top_vals / (top_vals.sum(-1, keepdims=True) + 1e-06)
        flat_sel = sel.reshape(-1)
        onehot = jax.nn.one_hot(flat_sel, E, dtype=jnp.int32)
        ranks = jnp.take_along_axis(jnp.cumsum(onehot, axis=0), flat_sel[:, None], axis=1)[:, 0] - 1
        valid = ranks < capacity
        sentinel = E * capacity
        slot = jnp.where(valid, flat_sel * capacity + ranks, sentinel)
        x_rep = jnp.repeat(xf, K, axis=0)
        padded = jnp.zeros((sentinel + 1, d), xf.dtype).at[slot].set(x_rep)
        padded = padded[:sentinel].reshape(E, capacity, d)
        h = jax.nn.gelu(jnp.einsum('ecd,edf->ecf', padded, w1), approximate=False)
        out_padded = jnp.einsum('ecf,efd->ecd', h, w2).reshape(sentinel, d)
        gathered = out_padded[jnp.minimum(slot, sentinel - 1)]
        gathered = jnp.where(valid[:, None], gathered, jnp.zeros((), xf.dtype))
        out = (gathered * weights.reshape(-1)[:, None]).reshape(T, K, d).sum(axis=1)
        return out.reshape(B, S, d)
    x = L0_attn_x
    xn = _layernorm(x, axis=-1)
    x = x + _L0_attn_ref(xn, L0_attn_fwd_a_logit, L0_attn_fwd_Wx, L0_attn_fwd_bx, L0_attn_fwd_Wgx, L0_attn_fwd_bgx, L0_attn_fwd_Wga, L0_attn_fwd_bga, L0_attn_fwd_Wo, L0_attn_fwd_bo, L0_attn_bwd_a_logit, L0_attn_bwd_Wx, L0_attn_bwd_bx, L0_attn_bwd_Wgx, L0_attn_bwd_bgx, L0_attn_bwd_Wga, L0_attn_bwd_bga, L0_attn_bwd_Wo, L0_attn_bwd_bo, L0_attn_ld_W, L0_attn_ld_b) + _L0_ffn_ref(xn, L0_ffn_gate_w, L0_ffn_w1, L0_ffn_w2)
    return x

_drawn_inputs = setup_inputs


def setup_inputs(seed=0):
    import zlib

    import numpy as np

    out = dict(_drawn_inputs(seed))
    spreads = {'L0_attn_fwd_bx': (0.0, 0.499),
     'L0_attn_fwd_bgx': (0.0, 2.0),
     'L0_attn_fwd_bga': (0.0, 2.0),
     'L0_attn_fwd_bo': (0.0, 0.505),
     'L0_attn_bwd_bx': (0.0, 0.589),
     'L0_attn_bwd_bgx': (0.0, 2.0),
     'L0_attn_bwd_bga': (0.0, 2.0),
     'L0_attn_bwd_bo': (0.0, 0.485),
     'L0_attn_ld_b': (0.0, 0.1)}
    factors = {'L0_attn_fwd_a_logit': 8.0,
     'L0_attn_fwd_Wgx': 3.429,
     'L0_attn_fwd_Wga': 5.374,
     'L0_attn_bwd_a_logit': 8.0,
     'L0_attn_bwd_Wgx': 3.51,
     'L0_attn_bwd_Wga': 5.241}
    for name, (base, spread) in spreads.items():
        noise = np.random.default_rng([zlib.crc32(name.encode()), seed]).standard_normal(out[name].shape)
        drawn = base * np.exp(spread * noise) if base else spread * noise
        out[name] = jnp.asarray(drawn.astype(out[name].dtype))
    for name, factor in factors.items():
        out[name] = (out[name] * factor).astype(out[name].dtype)
    return out
```

```python
from contextlib import ExitStack

import concourse.bass as bass
from concourse import mybir


def rglru_moe(nc, x_in, w_att, w_gate, cols_in, ldb_in, w1_in, w2_in, y_out):
    fp32 = mybir.dt.float32
    bf16 = mybir.dt.bfloat16
    i32 = mybir.dt.int32
    ALU = mybir.AluOpType
    ACT = mybir.ActivationFunctionType
    AX = mybir.AxisListType

    P = 128
    T = 2048
    SEQ = 256
    NT = T // P
    TC = 4
    NC = NT // TC
    CW = TC * P
    E = 16
    K = 2
    F = 256
    FB = F // P
    CAP = int(1.25 * T * K / E)
    NSLOT = E * CAP
    ROW = P + 2
    ID, WT = P, P + 1
    PT = 2 * CAP // P
    HALF = CAP - 2 * P
    NP = E // 2
    EPS = 1e-5
    W_EPS = 1e-6
    SAT = 17.5
    DROP = 8192.0
    NO_ID = 1 << 20
    OUT_OF_RACE = -1e30
    (A_LOGIT, B_X, B_GX, B_GA, B_O) = range(0, 10, 2)
    (W_X, W_GX, W_GA, W_O) = range(0, 8, 2)
    W_LD = 8

    slot_rows = nc.dram_tensor("slot_rows", [NSLOT, ROW], fp32, kind="Internal").ap()
    choice_rows = nc.dram_tensor("choice_rows", [T * K, P], fp32, kind="Internal").ap()

    ctx = ExitStack()
    with ctx:
        def sb(name, shape, dt=fp32):
            return ctx.enter_context(nc.sbuf_tensor(name, shape, dt))

        def sem(name):
            return ctx.enter_context(nc.semaphore(name))

        x = sb("x", [P, NT, P])
        rows = sb("rows", [P, NT, K, ROW])
        acc = sb("acc", [P, NT, P])
        xn_t = sb("xn_t", [P, T])
        xg_t = sb("xg_t", [P, T])
        proj = sb("proj", [P, 2, T])
        gate_x = sb("gate_x", [P, 2, T])
        decay = sb("decay", [P, 2, T])
        norm = sb("norm", [P, 2, T])
        watt = sb("watt", [P, 9, P])
        wgate = sb("wgate", [P, E])
        cols = sb("cols", [P, 10])
        ldb = sb("ldb", [P, P])
        consts = sb("consts", [P, 2])
        aexp = sb("aexp", [P, 2])
        bo_half = sb("bo_half", [P, 1])
        ident = sb("ident", [P, P])
        before = sb("before", [P, P], bf16)
        ones = sb("ones", [P, P], bf16)
        first_key = sb("first_key", [P, E])
        slot_base = sb("slot_base", [P, E])
        stats = sb("stats", [P, NT, 6])
        mv = sb("mv", [P, NT, 2])
        std = sb("std", [P, NT])
        rstd = sb("rstd", [P, NT])
        logit = sb("logit", [P, NT, E])
        logit2 = sb("logit2", [P, NT, E])
        best = sb("best", [P, K, NT])
        hit = sb("hit", [P, NT, E])
        key = sb("key", [P, NT])
        chosen = sb("chosen", [P, K, NT, E])
        mask = sb("mask", [P, NT, E], bf16)
        slot_e = sb("slot_e", [P, NT, E])
        slot_k = sb("slot_k", [P, K, NT, E])
        slot = sb("slot", [P, K, NT], i32)
        prob = sb("prob", [P, K, NT])
        prob_sum = sb("prob_sum", [P, NT])
        empty_row = sb("empty_row", [P, ROW])
        zeros = sb("zeros", [P, 8 * P])
        w1 = sb("w1", [P, 2, 2, F])
        w2 = sb("w2", [P, 2, 2, FB, P])
        xe = sb("xe", [P, 2, PT, ROW])
        xe_t = sb("xe_t", [P, 2, PT * P])
        hid = sb("hid", [P, 2, FB, 3 * P])
        ye = sb("ye", [P, 2, PT, P])
        back = sb("back", [P, NT, K * P])

        ps = ctx.enter_context(nc.psum_tensor("ps", [P, 8, 512], fp32))

        s_x = [sem(f"s_x{c}") for c in range(NC)]
        s_wts = sem("s_wts")
        s_empty = sem("s_empty")
        s_filled = sem("s_filled")
        s_cst = sem("s_cst")
        s_dcst = sem("s_dcst")
        s_pool = sem("s_pool")
        s_dve = sem("s_dve")
        s_act = sem("s_act")
        s_var = sem("s_var")
        s_std = sem("s_std")
        s_xn = sem("s_xn")
        s_xnt_ps = sem("s_xnt_ps")
        s_xnt = sem("s_xnt")
        s_xg = sem("s_xg")
        s_logits = sem("s_logits")
        s_mask = sem("s_mask")
        s_rank = sem("s_rank")
        s_best = sem("s_best")
        s_prob = sem("s_prob")
        s_aexp = sem("s_aexp")
        s_rows2 = sem("s_rows2")
        s_id = sem("s_id")
        s_rows = sem("s_rows")
        s_slot = sem("s_slot")
        s_sent = sem("s_sent")
        s_pj_ps = sem("s_pj_ps")
        s_pj = sem("s_pj")
        s_gate_ps = sem("s_gate_ps")
        s_gate = sem("s_gate")
        s_sq = sem("s_sq")
        s_norm = sem("s_norm")
        s_h = sem("s_h")
        s_o_ps = sem("s_o_ps")
        s_z = sem("s_z")
        s_g = sem("s_g")
        s_ld_ps = sem("s_ld_ps")
        s_ld = sem("s_ld")
        s_wexp = [sem(f"s_wexp{r}") for r in range(2)]
        s_xe = [sem(f"s_xe{r}") for r in range(2)]
        s_xet_ps = sem("s_xet_ps")
        s_xet = sem("s_xet")
        s_up = sem("s_up")
        s_gelu = sem("s_gelu")
        s_down = sem("s_down")
        s_y = sem("s_y")
        s_turn = sem("s_turn")
        s_back = [sem(f"s_back{r}") for r in range(2)]
        s_res = [sem(f"s_res{c}") for c in range(NC)]
        s_acc = sem("s_acc")
        s_out = sem("s_out")

        x_ap = x_in.rearrange("p (j d) -> p j d", d=P)
        out_ap = y_out.rearrange("p (j d) -> p j d", d=P)
        choice_ap = choice_rows.rearrange("(j p k) d -> p j (k d)", p=P, k=K)

        def bank(b, n=512):
            return ps[:, b, 0:n]

        def chunk(c):
            return slice(c * CW, (c + 1) * CW)

        GATE = [0, 1, 2, 3]
        PROJ = [4, 5]
        LOGIT, RANK = 6, 7
        logit_ps = ps[:, LOGIT, 0:NT * E].rearrange("p (j e) -> p j e", e=E)
        rank_ps = ps[:, RANK, 0:NT * E].rearrange("p (j e) -> p j e", e=E)
        XE_T, HID, RES = 0, [2, 4], [6, 7]
        xet_ps = ps[:, XE_T:XE_T + 2, :].rearrange("p b n -> p (b n)")[:, 0:PT * P]

        def pair_of(it, r):
            return it * 2 + r

        block = ctx.enter_context(nc.Block())

        @block.sync
        def _(sp):
            for c in range(NC):
                sp.dma_start(x[:, c * TC:(c + 1) * TC, :], x_ap[:, c * TC:(c + 1) * TC, :]).then_inc(s_x[c], 16)
            sp.wait_ge(s_empty, 3)
            sp.wait_ge(s_dcst, 2)
            sp.dma_start(slot_rows.rearrange("(p n) r -> p n r", p=P),
                         empty_row[:].unsqueeze(1).to_broadcast([P, NSLOT // P, ROW])).then_inc(s_filled, 16)
            sp.dma_start(choice_rows.rearrange("(p a n) d -> p a (n d)", p=P, n=8),
                         zeros[:].unsqueeze(1).to_broadcast([P, T * K // P // 8, 8 * P])).then_inc(s_filled, 16)

            def load_weights(it, r):
                q = pair_of(it, r)
                sp.dma_start(w1[:, r, :, :], w1_in[bass.ds(q * 2, 2), :, :].rearrange("e d f -> d e f")).then_inc(s_wexp[r], 16)
                sp.dma_start(w2[:, r, :, :, :].rearrange("p a b d -> p a (b d)"),
                             w2_in[bass.ds(q * 2, 2), :, :].rearrange("e p n -> p e n")).then_inc(s_wexp[r], 16)

            def load_rows(it, r):
                q = pair_of(it, r)
                sp.dma_start(xe[:, r, :, :], slot_rows[bass.ds(q * (PT * P), PT * P), :].rearrange(
                    "(n p) r -> p n r", p=P)).then_inc(s_xe[r], 16)

            for r in range(2):
                load_weights(0, r)
            sp.wait_ge(s_sent, 16 * NT * K)
            for r in range(2):
                load_rows(0, r)
            with sp.Fori(1, NP // 2) as it:
                for r in range(2):
                    sp.wait_ge(s_down, it * 4 + 2 * r)
                    load_weights(it, r)
                    sp.wait_ge(s_back[r], it * (16 * PT))
                    load_rows(it, r)
            for r in range(2):
                sp.wait_ge(s_back[r], 16 * PT * (NP // 2))
            for c in range(NC):
                sp.dma_start(back[:, c * TC:(c + 1) * TC, :], choice_ap[:, c * TC:(c + 1) * TC, :]).then_inc(s_res[c], 16)
            for c in range(NC):
                sp.wait_ge(s_acc, c + 1)
                sp.dma_start(out_ap[:, c * TC:(c + 1) * TC, :], acc[:, c * TC:(c + 1) * TC, :]).then_inc(s_out, 16)
            sp.wait_ge(s_out, 16 * NC)

        @block.gpsimd
        def _(pool):
            steps = [0]

            def then_wait(ins):
                steps[0] += 1
                ins.then_inc(s_pool, 1)
                pool.wait_ge(s_pool, steps[0])

            nc.gpsimd.memset(empty_row[:, 0:ID], 0.0).then_inc(s_empty, 1)
            nc.gpsimd.memset(empty_row[:, ID:WT].bitcast(i32), NO_ID).then_inc(s_empty, 1)
            nc.gpsimd.memset(empty_row[:, WT:ROW], 0.0).then_inc(s_empty, 1)
            then_wait(nc.gpsimd.memset(ident[:], 0.0))
            nc.gpsimd.affine_select(out=ident[:], in_=ident[:], compare_op=ALU.not_equal, fill=1.0, base=0,
                                    pattern=[[-1, P]], channel_multiplier=1).then_inc(s_cst, 1)
            then_wait(nc.gpsimd.memset(before[:], 0.0))
            nc.gpsimd.affine_select(out=before[:], in_=before[:], compare_op=ALU.is_ge, fill=1.0, base=0,
                                    pattern=[[-1, P]], channel_multiplier=1).then_inc(s_cst, 1)
            nc.gpsimd.iota(first_key[:], pattern=[[-1, E]], base=E, channel_multiplier=0,
                           allow_small_or_imprecise_dtypes=True).then_inc(s_cst, 1)
            nc.gpsimd.iota(slot_base[:], pattern=[[CAP, E]], base=0, channel_multiplier=0,
                           allow_small_or_imprecise_dtypes=True).then_inc(s_cst, 1)
            for k in range(K):
                nc.gpsimd.iota(rows[:, :, k, ID:WT].bitcast(i32), pattern=[[P * K, NT], [0, 1]], base=k,
                               channel_multiplier=K).then_inc(s_id, 1)
            for c in range(NC):
                pool.wait_ge(s_xn, TC * (c + 1))
                nc.gpsimd.tensor_copy(rows[:, c * TC:(c + 1) * TC, 1, 0:P],
                                      rows[:, c * TC:(c + 1) * TC, 0, 0:P]).then_inc(s_rows2, 1)
            pool.wait_ge(s_rows2, NC)
            pool.wait_ge(s_id, K)
            pool.wait_ge(s_slot, 1)
            pool.wait_ge(s_rows, 1)
            pool.wait_ge(s_filled, 32)
            for k in range(K):
                for j in range(NT):
                    pool.indirect_dma_start(slot_rows, bass.IndirectOffsetOnAxis(slot[:, k, j:j + 1], 0),
                                            rows[:, j, k, :], None, bounds_check=NSLOT - 1,
                                            oob_is_err=False).then_inc(s_sent, 16)

            last_id = pool.to_reg(T * K - 1)
            with pool.Fori(0, NP // 2) as it:
                for r in range(2):
                    for n in range(PT):
                        if n in (0, 2):
                            pool.wait_ge(s_y, it * 4 + 2 * r + (3 if n == 0 else 4))
                            pool.sem_inc(s_turn, 1)
                        pool.indirect_dma_start(
                            choice_rows, bass.IndirectOffsetOnAxis(xe[:, r, n, ID:WT].bitcast(i32), 0),
                            ye[:, r, n, :], None, bounds_check=last_id, oob_is_err=False).then_inc(s_back[r], 16)

        @block.scalar
        def _(act):
            act.dma_start(watt[:], w_att.rearrange("d (n f) -> d n f", f=P)).then_inc(s_wts, 16)
            act.dma_start(wgate[:], w_gate).then_inc(s_wts, 16)
            act.dma_start(cols[:], cols_in).then_inc(s_wts, 16)
            act.dma_start(ldb[:], ldb_in.partition_broadcast(P)).then_inc(s_wts, 16)

            def root(c):
                act.wait_ge(s_var, c + 1)
                nc.scalar.activation(std[:, c * TC:(c + 1) * TC], mv[:, c * TC:(c + 1) * TC, 1], ACT.Sqrt,
                                     bias=consts[:, 0:1]).then_inc(s_std, 1)

            def copy_out(c):
                act.wait_ge(s_xnt_ps, c + 1)
                nc.scalar.copy(xn_t[:, chunk(c)], bank(GATE[c])).then_inc(s_xnt, 1)

            act.wait_ge(s_dcst, 1)
            root(0)
            root(1)
            root(2)
            copy_out(0)
            root(3)
            for c in range(1, NC):
                copy_out(c)
            for c in range(NC):
                act.wait_ge(s_xnt, c + 1)
                nc.scalar.activation(xg_t[:, chunk(c)], xn_t[:, chunk(c)], ACT.Gelu_apprx_tanh).then_inc(s_xg, 1)
            act.wait_ge(s_wts, 64)
            nc.scalar.activation(aexp[:], cols[:, A_LOGIT:A_LOGIT + 2], ACT.Sigmoid).then_inc(s_aexp, 1)
            act.wait_ge(s_best, 2)
            nc.scalar.activation(prob[:], best[:], ACT.Sigmoid).then_inc(s_prob, 1)

            def project(c):
                for d in range(2):
                    act.wait_ge(s_pj_ps, 2 * c + d + 1)
                    nc.scalar.activation(proj[:, d, chunk(c)], bank(PROJ[d]), ACT.Identity,
                                         bias=cols[:, B_X + d:B_X + d + 1]).then_inc(s_pj, 1)

            project(0)
            for c in range(NC):
                for d in range(2):
                    for n, (dst, b) in enumerate(((gate_x, B_GX), (decay, B_GA))):
                        act.wait_ge(s_gate_ps, 4 * c + 2 * d + n + 1)
                        nc.scalar.activation(dst[:, d, chunk(c)], bank(GATE[2 * d + n]), ACT.Sigmoid,
                                             bias=cols[:, b + d:b + d + 1]).then_inc(s_gate, 1)
                if c + 1 < NC:
                    project(c + 1)
            for c in range(NC):
                act.wait_ge(s_sq, c + 1)
                nc.scalar.activation(norm[:, :, chunk(c)], norm[:, :, chunk(c)], ACT.Sqrt,
                                     scale=-1.0, bias=consts[:, 1:2]).then_inc(s_norm, 1)
            for c in range(NC):
                act.wait_ge(s_z, c + 1)
                nc.scalar.activation(xg_t[:, chunk(c)], xg_t[:, chunk(c)], ACT.Gelu_apprx_tanh,
                                     bias=bo_half[:]).then_inc(s_g, 1)
            act.sem_inc(s_gelu, 2)
            act.wait_ge(s_dcst, 2)
            with act.Fori(0, NP // 2) as it:
                for s in range(4):
                    o = s % 2
                    act.wait_ge(s_up, it * 4 + s + 5)
                    act.wait_ge(s_down, it * 4 + s + 1)
                    nc.scalar.activation(hid[:, o, :, o * HALF:o * HALF + CAP],
                                         ps[:, HID[o]:HID[o] + FB, 0:CAP], ACT.Gelu).then_inc(s_gelu, 1)

        @block.vector
        def _(dve):
            steps = [0]

            def then_wait(ins):
                steps[0] += 1
                ins.then_inc(s_dve, 1)
                dve.wait_ge(s_dve, steps[0])

            nc.vector.memset(consts[:, 0:1], EPS)
            nc.vector.memset(consts[:, 1:2], 1.0).then_inc(s_dcst, 1)
            nc.vector.memset(ones[:], 1.0)
            nc.vector.memset(zeros[:], 0.0)
            nc.vector.memset(hid[:, 0, :, CAP:3 * P], 0.0)
            nc.vector.memset(hid[:, 1, :, 0:HALF], 0.0).then_inc(s_dcst, 1)

            def moments(c):
                dve.wait_ge(s_x[c], 16)
                for j in range(c * TC, (c + 1) * TC):
                    last = nc.vector.bn_stats(stats[:, j, :], x[:, j, :])
                then_wait(last)
                for j in range(c * TC, (c + 1) * TC):
                    last = nc.vector.bn_aggr(mv[:, j, :], stats[:, j, :])
                last.then_inc(s_var, 1)

            def normalise(c):
                dve.wait_ge(s_std, c + 1)
                then_wait(nc.vector.reciprocal(rstd[:, c * TC:(c + 1) * TC], std[:, c * TC:(c + 1) * TC]))
                for j in range(c * TC, (c + 1) * TC):
                    nc.vector.tensor_scalar(rows[:, j, 0, 0:P], x[:, j, :], mv[:, j, 0:1], rstd[:, j:j + 1],
                                            ALU.subtract, ALU.mult).then_inc(s_xn, 1)

            moments(0)
            for c in range(NC):
                if c + 1 < NC:
                    moments(c + 1)
                normalise(c)

            dve.wait_ge(s_logits, 1)
            dve.wait_ge(s_cst, 4)
            then_wait(nc.vector.tensor_scalar(logit[:], logit_ps, SAT, None, ALU.min))
            keys = first_key[:].unsqueeze(1).to_broadcast([P, NT, E])
            for k, src in enumerate((logit, logit2)):
                nc.vector.tensor_reduce(best[:, k, :], src[:], AX.X, ALU.max).then_inc(s_best, 1)
                dve.wait_ge(s_best, k + 1)
                then_wait(nc.vector.tensor_tensor(hit[:], src[:], best[:, k, :].unsqueeze(2).to_broadcast([P, NT, E]),
                                                  ALU.is_equal))
                then_wait(nc.vector.tensor_tensor(hit[:], hit[:], keys, ALU.mult))
                then_wait(nc.vector.tensor_reduce(key[:], hit[:], AX.X, ALU.max))
                then_wait(nc.vector.tensor_tensor(chosen[:, k, :, :], keys,
                                                  key[:].unsqueeze(2).to_broadcast([P, NT, E]), ALU.is_equal))
                if k == 0:
                    then_wait(nc.vector.scalar_tensor_tensor(logit2[:], chosen[:, 0, :, :], OUT_OF_RACE, logit[:],
                                                             ALU.mult, ALU.add))
            nc.vector.tensor_tensor(mask[:], chosen[:, 0, :, :], chosen[:, 1, :, :], ALU.add).then_inc(s_mask, 1)
            dve.wait_ge(s_prob, 1)
            then_wait(nc.vector.scalar_tensor_tensor(prob_sum[:], prob[:, 0, :], W_EPS, prob[:, 1, :],
                                                     ALU.add, ALU.add))
            then_wait(nc.vector.reciprocal(prob_sum[:], prob_sum[:]))
            nc.vector.tensor_tensor(rows[:, :, :, WT].rearrange("p j k -> p k j"), prob[:],
                                    prob_sum[:].unsqueeze(1).to_broadcast([P, K, NT]), ALU.mult).then_inc(s_rows, 1)
            dve.wait_ge(s_rank, 1)
            then_wait(nc.vector.tensor_scalar(slot_e[:], rank_ps, float(CAP), DROP, ALU.is_ge, ALU.mult))
            then_wait(nc.vector.tensor_tensor(slot_e[:], slot_e[:], rank_ps, ALU.add))
            then_wait(nc.vector.tensor_tensor(slot_e[:], slot_e[:],
                                              slot_base[:].unsqueeze(1).to_broadcast([P, NT, E]), ALU.add))
            then_wait(nc.vector.tensor_tensor(slot_k[:], chosen[:],
                                              slot_e[:].unsqueeze(1).to_broadcast([P, K, NT, E]), ALU.mult))
            with nc.allow_low_precision("one whole number below 2^24 and zeros are added"):
                nc.vector.tensor_reduce(slot[:], slot_k[:], AX.X, ALU.add).then_inc(s_slot, 1)

            dve.wait_ge(s_aexp, 1)
            then_wait(nc.vector.tensor_tensor(bo_half[:], cols[:, B_O:B_O + 1], cols[:, B_O + 1:B_O + 2], ALU.add))
            then_wait(nc.vector.tensor_scalar(bo_half[:], bo_half[:], 0.5, None, ALU.mult))
            for c in range(NC):
                dve.wait_ge(s_gate, 4 * (c + 1))
                for d in range(2):
                    last = nc.vector.tensor_scalar(decay[:, d, chunk(c)], decay[:, d, chunk(c)], aexp[:, d:d + 1], 1.0,
                                                   ALU.mult, ALU.min)
                then_wait(last)
                nc.vector.tensor_tensor(norm[:, :, chunk(c)], decay[:, :, chunk(c)], decay[:, :, chunk(c)],
                                        ALU.mult).then_inc(s_sq, 1)
                dve.wait_ge(s_sq, c + 1)
                for s in range(c * CW, (c + 1) * CW, SEQ):
                    nc.vector.memset(decay[:, 0, s:s + 1], 0.0)
                    nc.vector.memset(decay[:, 1, s + SEQ - 1:s + SEQ], 0.0)
                then_wait(nc.vector.tensor_tensor(gate_x[:, :, chunk(c)], gate_x[:, :, chunk(c)], proj[:, :, chunk(c)],
                                                  ALU.mult))
            then_wait(nc.vector.tensor_tensor(acc[:], x[:], rows[:, :, 0, 0:P], ALU.add))
            then_wait(nc.vector.tensor_tensor(acc[:], acc[:], ldb[:].unsqueeze(1).to_broadcast([P, NT, P]), ALU.add))

            def combine(c):
                dve.wait_ge(s_o_ps, c + 1)
                nc.vector.scalar_tensor_tensor(xg_t[:, chunk(c)], bank(PROJ[c % 2]), 0.5, xn_t[:, chunk(c)],
                                               ALU.mult, ALU.add).then_inc(s_z, 1)

            def add_ld(c):
                dve.wait_ge(s_ld_ps, c + 1)
                a = acc[:, c * TC:(c + 1) * TC, :].rearrange("p j d -> p (j d)")
                nc.vector.tensor_tensor(a, a, bank(LOGIT + c % 2), ALU.add).then_inc(s_ld, 1)

            for c in range(NC):
                dve.wait_ge(s_norm, c + 1)
                then_wait(nc.vector.tensor_tensor(proj[:, :, chunk(c)], norm[:, :, chunk(c)], gate_x[:, :, chunk(c)],
                                                  ALU.mult))
                lo, hi = c * CW, (c + 1) * CW
                nc.vector.tensor_tensor_scan(gate_x[:, 0, lo:hi], decay[:, 0, lo:hi], proj[:, 0, lo:hi], 0.0,
                                             ALU.mult, ALU.add)
                rev = slice(hi - 1, lo - 1 if lo else None, -1)
                nc.vector.tensor_tensor_scan(gate_x[:, 1, rev], decay[:, 1, rev], proj[:, 1, rev], 0.0,
                                             ALU.mult, ALU.add).then_inc(s_h, 1)
                if c >= 1:
                    combine(c - 1)
                if c >= 2:
                    add_ld(c - 2)
            combine(NC - 1)
            add_ld(NC - 2)
            add_ld(NC - 1)

            dve.sem_inc(s_xet, 1)
            dve.sem_inc(s_y, 2)

            def transposed(it, r):
                dve.wait_ge(s_xet_ps, it * 2 + r + 1)
                dve.wait_ge(s_up, it * 4 + 2 * r + 2)
                nc.vector.tensor_copy(xe_t[:, r, :], xet_ps).then_inc(s_xet, 1)

            def results(it, s):
                r, o = s // 2, s % 2
                y_ps = bank(RES[o], 3 * P).rearrange("p (n d) -> p n d", d=P)
                dve.wait_ge(s_down, it * 4 + s + 3)
                full, part = (slice(0, 2), slice(2, 3)) if o == 0 else (slice(1, 3), slice(0, 1))
                tiles = slice(0, 2) if o == 0 else slice(3, 5)
                lanes = slice(0, HALF) if o == 0 else slice(HALF, P)
                nc.vector.tensor_tensor(ye[:, r, tiles, :], y_ps[:, full, :],
                                        xe[:, r, tiles, WT:ROW].to_broadcast([P, 2, P]), ALU.mult)
                nc.vector.tensor_tensor(ye[lanes, r, 2:3, :], y_ps[lanes, part, :],
                                        xe[lanes, r, 2:3, WT:ROW].to_broadcast([HALF, 1, P]), ALU.mult).then_inc(s_y, 1)

            transposed(0, 0)
            with dve.Fori(0, NP // 2 - 1) as it:
                transposed(it, 1)
                results(it, 0)
                results(it, 1)
                transposed(it + 1, 0)
                results(it, 2)
                results(it, 3)
            transposed(NP // 2 - 1, 1)
            for s in range(4):
                results(NP // 2 - 1, s)

            for c in range(NC):
                a = acc[:, c * TC:(c + 1) * TC, :]
                dve.wait_ge(s_res[c], 16)
                then_wait(nc.vector.tensor_tensor(a, a, back[:, c * TC:(c + 1) * TC, 0:P], ALU.add))
                nc.vector.tensor_tensor(a, a, back[:, c * TC:(c + 1) * TC, P:2 * P], ALU.add).then_inc(s_acc, 1)

        @block.tensor
        def _(pe):
            mm = nc.tensor.matmul

            def transpose_chunk(c):
                for i in range(TC):
                    j = c * TC + i
                    pe.wait_ge(s_xn, j + 1)
                    last = nc.tensor.transpose(ps[:, GATE[c], i * P:(i + 1) * P], rows[:, j, 0, 0:P], ident[:])
                last.then_inc(s_xnt_ps, 1)

            def logits_chunk(c):
                pe.wait_ge(s_xnt, c + 1)
                for j in range(c * TC, (c + 1) * TC):
                    last = mm(logit_ps[:, j, :], xn_t[:, j * P:(j + 1) * P], wgate[:], start=(j == 0), stop=True,
                              skip_group_check=True)
                if c == NC - 1:
                    last.then_inc(s_logits, 1)

            def projections(c):
                pe.wait_ge(s_xg, c + 1)
                if c:
                    pe.wait_ge(s_pj, 2 * c)
                for d in range(2):
                    mm(bank(PROJ[d]), watt[:, W_X + d, :], xg_t[:, chunk(c)], start=True, stop=True).then_inc(s_pj_ps, 1)

            def gates(c):
                if c:
                    pe.wait_ge(s_gate, 4 * c)
                for d in range(2):
                    pe.wait_ge(s_pj, 2 * c + d + 1)
                    for n, w in enumerate((W_GX, W_GA)):
                        mm(bank(GATE[2 * d + n]), watt[:, w + d, :], proj[:, d, chunk(c)],
                           start=True, stop=True).then_inc(s_gate_ps, 1)

            def ranks():
                pe.wait_ge(s_mask, 1)
                mm(rank_ps, before[:], mask[:], start=True, stop=False)
                for j in range(NT - 1):
                    n = NT - 1 - j
                    last = mm(rank_ps[:, j + 1:NT, :], ones[:], mask[:, j:j + 1, :].to_broadcast([P, n, E]),
                              start=False, stop=(j == NT - 2))
                last.then_inc(s_rank, 1)

            pe.wait_ge(s_cst, 4)
            pe.wait_ge(s_dcst, 2)
            pe.wait_ge(s_wts, 64)
            transpose_chunk(0)
            transpose_chunk(1)
            for c in range(NC):
                logits_chunk(c)
                if c + 2 < NC:
                    transpose_chunk(c + 2)
            projections(0)
            gates(0)
            projections(1)
            ranks()
            for c in range(1, NC):
                gates(c)
                if c + 1 < NC:
                    projections(c + 1)

            def outputs(c):
                pe.wait_ge(s_h, c + 1)
                if c >= 2:
                    pe.wait_ge(s_z, c - 1)
                else:
                    pe.wait_ge(s_pj, 2 * NC)
                mm(bank(PROJ[c % 2]), watt[:, W_O, :], gate_x[:, 0, chunk(c)], start=True, stop=False)
                mm(bank(PROJ[c % 2]), watt[:, W_O + 1, :], gate_x[:, 1, chunk(c)], start=False, stop=True).then_inc(s_o_ps, 1)

            def last_projection(c):
                pe.wait_ge(s_g, c + 1)
                if c >= 2:
                    pe.wait_ge(s_ld, c - 1)
                else:
                    pe.wait_ge(s_slot, 1)
                for i in range(TC):
                    j = c * TC + i
                    last = mm(ps[:, LOGIT + c % 2, i * P:(i + 1) * P], xg_t[:, j * P:(j + 1) * P], watt[:, W_LD, :],
                              start=(i == 0), stop=True, skip_group_check=True)
                last.then_inc(s_ld_ps, 1)

            outputs(0)
            for c in range(NC):
                if c + 1 < NC:
                    outputs(c + 1)
                last_projection(c)

            pe.sem_inc(s_up, 4)
            pe.sem_inc(s_down, 2)
            pe.wait_ge(s_gate, 4 * NC)
            pe.wait_ge(s_z, NC)
            pe.wait_ge(s_ld, NC)

            def transpose_rows(it, r):
                pe.wait_ge(s_xe[r], it * 16 + 16)
                pe.wait_ge(s_xet, it * 2 + r + 1)
                for n in range(PT):
                    last = nc.tensor.transpose(xet_ps[:, n * P:(n + 1) * P], xe[:, r, n, 0:P], ident[:])
                last.then_inc(s_xet_ps, 1)

            def up(it, s):
                r, o = s // 2, s % 2
                if o == 0:
                    pe.wait_ge(s_xet, it * 2 + r + 2)
                    pe.wait_ge(s_wexp[r], it * 32 + 32)
                pe.wait_ge(s_gelu, it * 4 + s + 1)
                for b in range(FB):
                    last = mm(ps[:, HID[o] + b, 0:CAP], w1[:, r, o, b * P:(b + 1) * P],
                              xe_t[:, r, o * CAP:(o + 1) * CAP], start=True, stop=True)
                last.then_inc(s_up, 1)

            def down(it, s):
                r, o = s // 2, s % 2
                pe.wait_ge(s_gelu, it * 4 + s + 3)
                pe.wait_ge(s_y, it * 4 + s + 1)
                for n in range(3):
                    for b in range(FB):
                        last = mm(ps[:, RES[o], n * P:(n + 1) * P], hid[:, o, b, n * P:(n + 1) * P],
                                  w2[:, r, o, b, :], start=(b == 0), stop=(b == FB - 1))
                last.then_inc(s_down, 1)

            transpose_rows(0, 0)
            up(0, 0)
            with pe.Fori(0, NP // 2 - 1) as it:
                transpose_rows(it, 1)
                up(it, 1)
                down(it, 0)
                up(it, 2)
                down(it, 1)
                transpose_rows(it + 1, 0)
                up(it, 3)
                down(it, 2)
                up(it + 1, 0)
                down(it, 3)
            it = NP // 2 - 1
            transpose_rows(it, 1)
            up(it, 1)
            down(it, 0)
            up(it, 2)
            down(it, 1)
            up(it, 3)
            down(it, 2)
            down(it, 3)


def kernel(**inputs):
    import numpy as np
    import concourse.bacc as bacc
    from concourse.bass_utils import run_bass_kernel_spmd

    fp32 = mybir.dt.float32
    a = {k: np.asarray(v) for k, v in inputs.items()}
    att = {k[len("L0_attn_"):]: v for k, v in a.items() if k.startswith("L0_attn_")}
    both = [f"{d}_{n}" for n in ("Wx", "Wgx", "Wga", "Wo") for d in ("fwd", "bwd")]
    cols = [f"{d}_{n}" for n in ("a_logit", "bx", "bgx", "bga", "bo") for d in ("fwd", "bwd")]
    x = att["x"]
    arrays = {
        "x_d": x.reshape(16, 128, 128).transpose(1, 0, 2).reshape(128, 2048),
        "w_att_d": np.concatenate([att[n] for n in both] + [att["ld_W"]], axis=1),
        "w_gate_d": a["L0_ffn_gate_w"].T,
        "cols_d": np.stack([att[n] for n in cols], axis=1),
        "ldb_d": att["ld_b"].reshape(128),
        "w1_d": a["L0_ffn_w1"],
        "w2_d": a["L0_ffn_w2"].reshape(16, 2, 128, 128).transpose(0, 2, 1, 3).reshape(16, 128, 256),
    }
    arrays = {k: np.ascontiguousarray(v) for k, v in arrays.items()}
    nc = bacc.Bacc("TRN2", target_bir_lowering=False, num_devices=1)
    aps = [nc.dram_tensor(k, v.shape, fp32, kind="ExternalInput").ap() for k, v in arrays.items()]
    out = nc.dram_tensor("out_d", (128, 2048), fp32, kind="ExternalOutput").ap()
    rglru_moe(nc, *aps, out)
    r = run_bass_kernel_spmd(nc, [arrays], core_ids=[0])
    y = r.results[0]["out_d"]
    return y.reshape(128, 16, 128).transpose(1, 0, 2).reshape(x.shape)
```

```python
from contextlib import ExitStack

import concourse.bass as bass
from concourse import mybir


def rglru_moe(nc, x_in, w_att, w_gate, cols_in, ldb_in, w1_in, w2_in, y_out):
    fp32 = mybir.dt.float32
    bf16 = mybir.dt.bfloat16
    i32 = mybir.dt.int32
    ALU = mybir.AluOpType
    ACT = mybir.ActivationFunctionType
    AX = mybir.AxisListType

    P = 128
    T = 2048
    SEQ = 256
    NT = T // P
    TC = 4
    NC = NT // TC
    HT = NT // 2
    CW = TC * P
    E = 16
    K = 2
    F = 256
    FB = F // P
    CAP = int(1.25 * T * K / E)
    NSLOT = E * CAP
    ROW = P + 2
    ID, WT = P, P + 1
    PT = 2 * CAP // P
    HALF = CAP - 2 * P
    NP = E // 2
    EPS = 1e-5
    W_EPS = 1e-6
    SAT = 17.5
    DROP = 8192.0
    NO_ID = 1 << 20
    OUT_OF_RACE = -1e30
    (A_LOGIT, B_X, B_GX, B_GA, B_O) = range(0, 10, 2)
    (W_X, W_GX, W_GA, W_O) = range(0, 8, 2)
    W_LD = 8

    slot_rows = nc.dram_tensor("slot_rows", [NSLOT, ROW], fp32, kind="Internal").ap()
    choice_rows = nc.dram_tensor("choice_rows", [T * K, P], fp32, kind="Internal").ap()

    ctx = ExitStack()
    with ctx:
        def sb(name, shape, dt=fp32):
            return ctx.enter_context(nc.sbuf_tensor(name, shape, dt))

        def sem(name):
            return ctx.enter_context(nc.semaphore(name))

        x = sb("x", [P, NT, P])
        rows = sb("rows", [P, NT, K, ROW])
        acc = sb("acc", [P, NT, P])
        xn_t = sb("xn_t", [P, T])
        xg_t = sb("xg_t", [P, T])
        proj = sb("proj", [P, 2, T])
        gate_x = sb("gate_x", [P, 2, T])
        decay = sb("decay", [P, 2, T])
        norm = sb("norm", [P, 2, T])
        watt = sb("watt", [P, 9, P])
        wgate = sb("wgate", [P, E])
        cols = sb("cols", [P, 10])
        ldb = sb("ldb", [P, P])
        consts = sb("consts", [P, 2])
        aexp = sb("aexp", [P, 2])
        bo_half = sb("bo_half", [P, 1])
        ident = sb("ident", [P, P])
        before = sb("before", [P, P], bf16)
        ones = sb("ones", [P, P], bf16)
        first_key = sb("first_key", [P, E])
        slot_base = sb("slot_base", [1, HT, E], bf16)
        slot_end = sb("slot_end", [P, E])
        stats = sb("stats", [P, NT, 6])
        mv = sb("mv", [P, NT, 2])
        std = sb("std", [P, NT])
        rstd = sb("rstd", [P, NT])
        logit = sb("logit", [P, NT, E])
        logit2 = sb("logit2", [P, NT, E])
        best = sb("best", [P, 2, K, HT])
        hit = sb("hit", [P, HT, E])
        key = sb("key", [P, HT])
        chosen = sb("chosen", [P, 2, K, HT, E])
        mask = sb("mask", [P, NT, E], bf16)
        over = sb("over", [P, HT, E])
        slot_e = sb("slot_e", [P, HT, E])
        slot_k = sb("slot_k", [P, K, HT, E])
        slot = sb("slot", [P, 2, K, HT], i32)
        prob = sb("prob", [P, 2, K, HT])
        prob_sum = sb("prob_sum", [P, HT])
        empty_row = sb("empty_row", [P, ROW])
        zeros = sb("zeros", [P, 8 * P])
        w1 = sb("w1", [P, 2, 2, F])
        w2 = sb("w2", [P, 2, 2, FB, P])
        xe = sb("xe", [P, 2, PT, ROW])
        tags = sb("tags", [P, 2, PT, 2])
        xe_t = sb("xe_t", [P, 2, PT * P])
        hid = sb("hid", [P, 2, FB, 3 * P])
        ye = sb("ye", [P, 2, PT, P])
        back = sb("back", [P, NT, K * P])

        ps = ctx.enter_context(nc.psum_tensor("ps", [P, 8, 512], fp32))

        s_x = [sem(f"s_x{c}") for c in range(NC)]
        s_wts = sem("s_wts")
        s_wgate = sem("s_wgate")
        s_tags = sem("s_tags")
        s_tags_free = sem("s_tags_free")
        s_empty = sem("s_empty")
        s_filled = sem("s_filled")
        s_cst = sem("s_cst")
        s_dcst = sem("s_dcst")
        s_pool = sem("s_pool")
        s_dve = sem("s_dve")
        s_act = sem("s_act")
        s_var = sem("s_var")
        s_std = sem("s_std")
        s_xn = sem("s_xn")
        s_xnt_ps = sem("s_xnt_ps")
        s_xnt = sem("s_xnt")
        s_xg = sem("s_xg")
        s_logits = sem("s_logits")
        s_mask = sem("s_mask")
        s_rank = sem("s_rank")
        s_best = sem("s_best")
        s_prob = sem("s_prob")
        s_aexp = sem("s_aexp")
        s_rows2 = sem("s_rows2")
        s_id = sem("s_id")
        s_rows = sem("s_rows")
        s_slot = sem("s_slot")
        s_sent = sem("s_sent")
        s_pj_ps = sem("s_pj_ps")
        s_pj = sem("s_pj")
        s_gate_ps = sem("s_gate_ps")
        s_gate = sem("s_gate")
        s_a = sem("s_a")
        s_sq = sem("s_sq")
        s_norm = sem("s_norm")
        s_h = sem("s_h")
        s_o_ps = sem("s_o_ps")
        s_z = sem("s_z")
        s_g = sem("s_g")
        s_ld_ps = sem("s_ld_ps")
        s_ld = sem("s_ld")
        s_wexp = [sem(f"s_wexp{r}") for r in range(2)]
        s_xe = [sem(f"s_xe{r}") for r in range(2)]
        s_xet_ps = sem("s_xet_ps")
        s_xet = sem("s_xet")
        s_up = sem("s_up")
        s_gelu = sem("s_gelu")
        s_down = sem("s_down")
        s_y = sem("s_y")
        s_turn = sem("s_turn")
        s_back = [sem(f"s_back{r}") for r in range(2)]
        s_res = [sem(f"s_res{c}") for c in range(NC)]
        s_acc = sem("s_acc")
        s_out = sem("s_out")

        x_ap = x_in.rearrange("p (j d) -> p j d", d=P)
        out_ap = y_out.rearrange("p (j d) -> p j d", d=P)
        choice_ap = choice_rows.rearrange("(j p k) d -> p j (k d)", p=P, k=K)

        def bank(b, n=512):
            return ps[:, b, 0:n]

        def chunk(c):
            return slice(c * CW, (c + 1) * CW)

        GATE = [0, 1, 2, 3]
        PROJ = [4, 5]
        ROUTE = [6, 7]
        logit_ps = [ps[:, b, 0:HT * E].rearrange("p (j e) -> p j e", e=E) for b in ROUTE]
        rank_ps = [ps[:, b, HT * E:2 * HT * E].rearrange("p (j e) -> p j e", e=E) for b in ROUTE]
        XE_T, HID, RES = 0, [2, 4], [6, 7]
        xet_ps = ps[:, XE_T:XE_T + 2, :].rearrange("p b n -> p (b n)")[:, 0:PT * P]

        def half(h):
            return slice(h * HT, (h + 1) * HT)

        def pair_of(it, r):
            return it * 2 + r

        block = ctx.enter_context(nc.Block())

        @block.sync
        def _(sp):
            for c in range(0, NC, 2):
                sp.dma_start(x[:, c * TC:(c + 1) * TC, :], x_ap[:, c * TC:(c + 1) * TC, :]).then_inc(s_x[c], 16)
            sp.dma_start(wgate[:], w_gate).then_inc(s_wgate, 16)
            sp.wait_ge(s_empty, 3)
            sp.wait_ge(s_dcst, 2)
            sp.dma_start(slot_rows.rearrange("(p n) r -> p n r", p=P),
                         empty_row[:].unsqueeze(1).to_broadcast([P, NSLOT // P, ROW])).then_inc(s_filled, 16)
            sp.dma_start(choice_rows.rearrange("(p a n) d -> p a (n d)", p=P, n=8),
                         zeros[:].unsqueeze(1).to_broadcast([P, T * K // P // 8, 8 * P])).then_inc(s_filled, 16)

            def load_weights(it, r):
                q = pair_of(it, r)
                sp.dma_start(w1[:, r, :, :], w1_in[bass.ds(q * 2, 2), :, :].rearrange("e d f -> d e f")).then_inc(s_wexp[r], 16)
                sp.dma_start(w2[:, r, :, :, :].rearrange("p a b d -> p a (b d)"),
                             w2_in[bass.ds(q * 2, 2), :, :].rearrange("e p n -> p e n")).then_inc(s_wexp[r], 16)

            def load_rows(it, r):
                q = pair_of(it, r)
                sp.dma_start(xe[:, r, :, :], slot_rows[bass.ds(q * (PT * P), PT * P), :].rearrange(
                    "(n p) r -> p n r", p=P)).then_inc(s_xe[r], 16)

            for r in range(2):
                load_weights(0, r)
            sp.wait_ge(s_sent, 16 * NT * K)
            for r in range(2):
                load_rows(0, r)
            sp.sem_inc(s_tags_free, 2)
            sp.wait_ge(s_tags, 1)
            load_rows(1, 0)

            def refill(it, r, rows_too=True):
                sp.wait_ge(s_down, it * 4 + 2 * r)
                load_weights(it, r)
                if rows_too:
                    sp.wait_ge(s_tags, it * 2 + r)
                    load_rows(it + r, 1 - r)
                sp.wait_ge(s_back[r], it * (16 * PT))
                sp.sem_inc(s_tags_free, 1)

            with sp.Fori(1, NP // 2 - 1) as it:
                refill(it, 0)
                refill(it, 1)
            refill(NP // 2 - 1, 0)
            refill(NP // 2 - 1, 1, rows_too=False)
            for r in range(2):
                sp.wait_ge(s_back[r], 16 * PT * (NP // 2))
            for c in range(NC):
                sp.dma_start(back[:, c * TC:(c + 1) * TC, :], choice_ap[:, c * TC:(c + 1) * TC, :]).then_inc(s_res[c], 16)
            for c in range(NC):
                sp.wait_ge(s_acc, c + 1)
                sp.dma_start(out_ap[:, c * TC:(c + 1) * TC, :], acc[:, c * TC:(c + 1) * TC, :]).then_inc(s_out, 16)
            sp.wait_ge(s_out, 16 * NC)

        @block.gpsimd
        def _(pool):
            steps = [0]

            def then_wait(ins):
                steps[0] += 1
                ins.then_inc(s_pool, 1)
                pool.wait_ge(s_pool, steps[0])

            nc.gpsimd.memset(empty_row[:, 0:ID], 0.0).then_inc(s_empty, 1)
            nc.gpsimd.memset(empty_row[:, ID:WT].bitcast(i32), NO_ID).then_inc(s_empty, 1)
            nc.gpsimd.memset(empty_row[:, WT:ROW], 0.0).then_inc(s_empty, 1)
            then_wait(nc.gpsimd.memset(ident[:], 0.0))
            nc.gpsimd.affine_select(out=ident[:], in_=ident[:], compare_op=ALU.not_equal, fill=1.0, base=0,
                                    pattern=[[-1, P]], channel_multiplier=1).then_inc(s_cst, 1)
            then_wait(nc.gpsimd.memset(before[:], 0.0))
            nc.gpsimd.affine_select(out=before[:], in_=before[:], compare_op=ALU.is_ge, fill=1.0, base=0,
                                    pattern=[[-1, P]], channel_multiplier=1).then_inc(s_cst, 1)
            nc.gpsimd.iota(first_key[:], pattern=[[-1, E]], base=E, channel_multiplier=0,
                           allow_small_or_imprecise_dtypes=True).then_inc(s_cst, 1)
            nc.gpsimd.iota(slot_base[:], pattern=[[0, HT], [CAP, E]], base=0, channel_multiplier=0,
                           allow_small_or_imprecise_dtypes=True).then_inc(s_cst, 1)
            nc.gpsimd.iota(slot_end[:], pattern=[[CAP, E]], base=CAP, channel_multiplier=0,
                           allow_small_or_imprecise_dtypes=True).then_inc(s_cst, 1)
            nc.gpsimd.memset(ones[:], 1.0).then_inc(s_cst, 1)
            for k in range(K):
                nc.gpsimd.iota(rows[:, :, k, ID:WT].bitcast(i32), pattern=[[P * K, NT], [0, 1]], base=k,
                               channel_multiplier=K).then_inc(s_id, 1)
            for c in range(NC):
                pool.wait_ge(s_xn, TC * (c + 1))
                nc.gpsimd.tensor_copy(rows[:, c * TC:(c + 1) * TC, 1, 0:P],
                                      rows[:, c * TC:(c + 1) * TC, 0, 0:P]).then_inc(s_rows2, 1)
            pool.wait_ge(s_rows2, NC)
            pool.wait_ge(s_id, K)
            pool.wait_ge(s_filled, 32)
            for h in range(2):
                pool.wait_ge(s_slot, h + 1)
                pool.wait_ge(s_rows, h + 1)
                for j in range(HT):
                    for k in range(K):
                        pool.indirect_dma_start(slot_rows, bass.IndirectOffsetOnAxis(slot[:, h, k, j:j + 1], 0),
                                                rows[:, h * HT + j, k, :], None, bounds_check=NSLOT - 1,
                                                oob_is_err=False).then_inc(s_sent, 16)

            last_id = pool.to_reg(T * K - 1)
            with pool.Fori(0, NP // 2) as it:
                for r in range(2):
                    for n in range(PT):
                        if n in (0, 2):
                            pool.wait_ge(s_y, it * 4 + 2 * r + (3 if n == 0 else 4))
                            pool.sem_inc(s_turn, 1)
                        pool.indirect_dma_start(
                            choice_rows, bass.IndirectOffsetOnAxis(tags[:, r, n, 0:1].bitcast(i32), 0),
                            ye[:, r, n, :], None, bounds_check=last_id, oob_is_err=False).then_inc(s_back[r], 16)

        @block.scalar
        def _(act):
            for c in range(1, NC, 2):
                act.dma_start(x[:, c * TC:(c + 1) * TC, :], x_ap[:, c * TC:(c + 1) * TC, :]).then_inc(s_x[c], 16)
            act.dma_start(watt[:], w_att.rearrange("d (n f) -> d n f", f=P)).then_inc(s_wts, 16)
            act.dma_start(cols[:], cols_in).then_inc(s_wts, 16)
            act.dma_start(ldb[:], ldb_in.partition_broadcast(P)).then_inc(s_wts, 16)

            def root(c):
                act.wait_ge(s_var, c + 1)
                nc.scalar.activation(std[:, c * TC:(c + 1) * TC], mv[:, c * TC:(c + 1) * TC, 1], ACT.Sqrt,
                                     bias=consts[:, 0:1]).then_inc(s_std, 1)

            def copy_out(c):
                act.wait_ge(s_xnt_ps, c + 1)
                nc.scalar.copy(xn_t[:, chunk(c)], bank(GATE[c])).then_inc(s_xnt, 1)

            act.wait_ge(s_dcst, 1)
            root(0)
            root(1)
            root(2)
            copy_out(0)
            root(3)
            for c in range(1, NC):
                copy_out(c)
            for c in range(NC):
                act.wait_ge(s_xnt, c + 1)
                nc.scalar.activation(xg_t[:, chunk(c)], xn_t[:, chunk(c)], ACT.Gelu_apprx_tanh).then_inc(s_xg, 1)
            act.wait_ge(s_wts, 48)
            nc.scalar.activation(aexp[:], cols[:, A_LOGIT:A_LOGIT + 2], ACT.Sigmoid).then_inc(s_aexp, 1)

            def probabilities(h):
                act.wait_ge(s_best, 2 * (h + 1))
                nc.scalar.activation(prob[:, h, :, :], best[:, h, :, :], ACT.Sigmoid).then_inc(s_prob, 1)

            probabilities(0)

            def project(c):
                for d in range(2):
                    act.wait_ge(s_pj_ps, 2 * c + d + 1)
                    nc.scalar.activation(proj[:, d, chunk(c)], bank(PROJ[d]), ACT.Identity,
                                         bias=cols[:, B_X + d:B_X + d + 1]).then_inc(s_pj, 1)

            def gates(c):
                for d in range(2):
                    for n, (dst, b) in enumerate(((gate_x, B_GX), (decay, B_GA))):
                        act.wait_ge(s_gate_ps, 4 * c + 2 * d + n + 1)
                        nc.scalar.activation(dst[:, d, chunk(c)], bank(GATE[2 * d + n]), ACT.Sigmoid,
                                             bias=cols[:, b + d:b + d + 1]).then_inc(s_gate, 1)

            def square(c):
                act.wait_ge(s_a, c + 1)
                nc.scalar.activation(norm[:, :, chunk(c)], decay[:, :, chunk(c)], ACT.Square).then_inc(s_sq, 1)

            def norms(c):
                act.wait_ge(s_sq, c + 1)
                nc.scalar.activation(norm[:, :, chunk(c)], norm[:, :, chunk(c)], ACT.Sqrt,
                                     scale=-1.0, bias=consts[:, 1:2]).then_inc(s_norm, 1)

            project(0)
            gates(0)
            probabilities(1)
            project(1)
            gates(1)
            square(0)
            project(2)
            square(1)
            norms(0)
            norms(1)
            gates(2)
            project(3)
            gates(3)
            square(2)
            square(3)
            norms(2)
            norms(3)
            for c in range(NC):
                act.wait_ge(s_z, c + 1)
                nc.scalar.activation(xg_t[:, chunk(c)], xg_t[:, chunk(c)], ACT.Gelu_apprx_tanh,
                                     bias=bo_half[:]).then_inc(s_g, 1)
            act.sem_inc(s_gelu, 2)
            act.wait_ge(s_dcst, 2)
            with act.Fori(0, NP // 2) as it:
                for s in range(4):
                    o = s % 2
                    act.wait_ge(s_up, it * 4 + s + 5)
                    act.wait_ge(s_down, it * 4 + s + 1)
                    nc.scalar.activation(hid[:, o, :, o * HALF:o * HALF + CAP],
                                         ps[:, HID[o]:HID[o] + FB, 0:CAP], ACT.Gelu).then_inc(s_gelu, 1)

        @block.vector
        def _(dve):
            steps = [0]

            def then_wait(ins):
                steps[0] += 1
                ins.then_inc(s_dve, 1)
                dve.wait_ge(s_dve, steps[0])

            nc.vector.memset(consts[:, 0:1], EPS)
            nc.vector.memset(consts[:, 1:2], 1.0).then_inc(s_dcst, 1)
            nc.vector.memset(zeros[:], 0.0)
            nc.vector.memset(hid[:, 0, :, CAP:3 * P], 0.0)
            nc.vector.memset(hid[:, 1, :, 0:HALF], 0.0).then_inc(s_dcst, 1)

            def moments(c):
                dve.wait_ge(s_x[c], 16)
                for j in range(c * TC, (c + 1) * TC):
                    last = nc.vector.bn_stats(stats[:, j, :], x[:, j, :])
                then_wait(last)
                for j in range(c * TC, (c + 1) * TC):
                    last = nc.vector.bn_aggr(mv[:, j, :], stats[:, j, :])
                last.then_inc(s_var, 1)

            def normalise(c):
                dve.wait_ge(s_std, c + 1)
                then_wait(nc.vector.reciprocal(rstd[:, c * TC:(c + 1) * TC], std[:, c * TC:(c + 1) * TC]))
                for j in range(c * TC, (c + 1) * TC):
                    nc.vector.tensor_scalar(rows[:, j, 0, 0:P], x[:, j, :], mv[:, j, 0:1], rstd[:, j:j + 1],
                                            ALU.subtract, ALU.mult).then_inc(s_xn, 1)

            moments(0)
            for c in range(NC):
                if c + 1 < NC:
                    moments(c + 1)
                normalise(c)

            def choose(h):
                js = half(h)
                shape = [P, HT, E]
                keys = first_key[:].unsqueeze(1).to_broadcast(shape)
                dve.wait_ge(s_logits, h + 1)
                then_wait(nc.vector.tensor_scalar(logit[:, js, :], logit_ps[h], SAT, None, ALU.min))
                for k, src in enumerate((logit, logit2)):
                    nc.vector.tensor_reduce(best[:, h, k, :], src[:, js, :], AX.X, ALU.max).then_inc(s_best, 1)
                    dve.wait_ge(s_best, 2 * h + k + 1)
                    then_wait(nc.vector.tensor_tensor(hit[:], src[:, js, :],
                                                      best[:, h, k, :].unsqueeze(2).to_broadcast(shape), ALU.is_equal))
                    then_wait(nc.vector.tensor_tensor(hit[:], hit[:], keys, ALU.mult))
                    then_wait(nc.vector.tensor_reduce(key[:], hit[:], AX.X, ALU.max))
                    then_wait(nc.vector.tensor_tensor(chosen[:, h, k, :, :], keys,
                                                      key[:].unsqueeze(2).to_broadcast(shape), ALU.is_equal))
                    if k == 0:
                        then_wait(nc.vector.scalar_tensor_tensor(logit2[:, js, :], chosen[:, h, 0, :, :], OUT_OF_RACE,
                                                                 logit[:, js, :], ALU.mult, ALU.add))
                nc.vector.tensor_tensor(mask[:, js, :], chosen[:, h, 0, :, :], chosen[:, h, 1, :, :],
                                        ALU.add).then_inc(s_mask, 1)

            def place(h):
                js = half(h)
                dve.wait_ge(s_rank, h + 1)
                then_wait(nc.vector.tensor_tensor(over[:], rank_ps[h],
                                                  slot_end[:].unsqueeze(1).to_broadcast([P, HT, E]), ALU.is_ge))
                then_wait(nc.vector.scalar_tensor_tensor(slot_e[:], over[:], DROP, rank_ps[h],
                                                         ALU.mult, ALU.add))
                then_wait(nc.vector.tensor_tensor(slot_k[:], chosen[:, h, :, :, :],
                                                  slot_e[:].unsqueeze(1).to_broadcast([P, K, HT, E]), ALU.mult))
                with nc.allow_low_precision("one whole number below 2^24 and zeros are added"):
                    nc.vector.tensor_reduce(slot[:, h, :, :], slot_k[:], AX.X, ALU.add).then_inc(s_slot, 1)
                dve.wait_ge(s_prob, h + 1)
                then_wait(nc.vector.scalar_tensor_tensor(prob_sum[:], prob[:, h, 0, :], W_EPS, prob[:, h, 1, :],
                                                         ALU.add, ALU.add))
                then_wait(nc.vector.reciprocal(prob_sum[:], prob_sum[:]))
                nc.vector.tensor_tensor(rows[:, js, :, WT].rearrange("p j k -> p k j"), prob[:, h, :, :],
                                        prob_sum[:].unsqueeze(1).to_broadcast([P, K, HT]), ALU.mult).then_inc(s_rows, 1)

            dve.wait_ge(s_cst, 6)
            for h in range(2):
                choose(h)
                place(h)

            dve.wait_ge(s_aexp, 1)
            then_wait(nc.vector.tensor_tensor(bo_half[:], cols[:, B_O:B_O + 1], cols[:, B_O + 1:B_O + 2], ALU.add))
            then_wait(nc.vector.tensor_scalar(bo_half[:], bo_half[:], 0.5, None, ALU.mult))

            def decays(c):
                dve.wait_ge(s_gate, 4 * (c + 1))
                for d in range(2):
                    last = nc.vector.tensor_scalar(decay[:, d, chunk(c)], decay[:, d, chunk(c)], aexp[:, d:d + 1], 1.0,
                                                   ALU.mult, ALU.min)
                last.then_inc(s_a, 1)
                nc.vector.tensor_tensor(gate_x[:, :, chunk(c)], gate_x[:, :, chunk(c)], proj[:, :, chunk(c)], ALU.mult)
                dve.wait_ge(s_sq, c + 1)
                for s in range(c * CW, (c + 1) * CW, SEQ):
                    nc.vector.memset(decay[:, 0, s:s + 1], 0.0)
                    last = nc.vector.memset(decay[:, 1, s + SEQ - 1:s + SEQ], 0.0)
                then_wait(last)

            def scan(c):
                dve.wait_ge(s_norm, c + 1)
                then_wait(nc.vector.tensor_tensor(proj[:, :, chunk(c)], norm[:, :, chunk(c)], gate_x[:, :, chunk(c)],
                                                  ALU.mult))
                lo, hi = c * CW, (c + 1) * CW
                nc.vector.tensor_tensor_scan(gate_x[:, 0, lo:hi], decay[:, 0, lo:hi], proj[:, 0, lo:hi], 0.0,
                                             ALU.mult, ALU.add)
                rev = slice(hi - 1, lo - 1 if lo else None, -1)
                nc.vector.tensor_tensor_scan(gate_x[:, 1, rev], decay[:, 1, rev], proj[:, 1, rev], 0.0,
                                             ALU.mult, ALU.add).then_inc(s_h, 1)

            def combine(c):
                dve.wait_ge(s_o_ps, c + 1)
                nc.vector.scalar_tensor_tensor(xg_t[:, chunk(c)], bank(PROJ[c % 2]), 0.5, xn_t[:, chunk(c)],
                                               ALU.mult, ALU.add).then_inc(s_z, 1)

            def add_ld(c):
                dve.wait_ge(s_ld_ps, c + 1)
                a = acc[:, c * TC:(c + 1) * TC, :].rearrange("p j d -> p (j d)")
                nc.vector.tensor_tensor(a, x[:, c * TC:(c + 1) * TC, :].rearrange("p j d -> p (j d)"),
                                        bank(ROUTE[c % 2]), ALU.add).then_inc(s_ld, 1)

            decays(0)
            decays(1)
            scan(0)
            scan(1)
            decays(2)
            decays(3)
            scan(2)
            combine(0)
            combine(1)
            scan(3)
            combine(2)
            add_ld(0)
            add_ld(1)
            combine(3)
            add_ld(2)
            add_ld(3)

            dve.sem_inc(s_xet, 1)
            dve.sem_inc(s_y, 2)

            def transposed(it, r):
                dve.wait_ge(s_xet_ps, it * 2 + r + 1)
                dve.wait_ge(s_up, it * 4 + 2 * r + 2)
                nc.vector.tensor_copy(xe_t[:, r, :], xet_ps).then_inc(s_xet, 1)

            def results(it, s):
                r, o = s // 2, s % 2
                y_ps = bank(RES[o], 3 * P).rearrange("p (n d) -> p n d", d=P)
                dve.wait_ge(s_down, it * 4 + s + 3)
                full, part = (slice(0, 2), slice(2, 3)) if o == 0 else (slice(1, 3), slice(0, 1))
                tiles = slice(0, 2) if o == 0 else slice(3, 5)
                lanes = slice(0, HALF) if o == 0 else slice(HALF, P)
                nc.vector.tensor_tensor(ye[:, r, tiles, :], y_ps[:, full, :],
                                        tags[:, r, tiles, 1:2].to_broadcast([P, 2, P]), ALU.mult)
                nc.vector.tensor_tensor(ye[lanes, r, 2:3, :], y_ps[lanes, part, :],
                                        tags[lanes, r, 2:3, 1:2].to_broadcast([HALF, 1, P]), ALU.mult).then_inc(s_y, 1)

            def keep_tags(it, r):
                dve.wait_ge(s_tags_free, it * 2 + r + 1)
                ins = nc.vector.tensor_copy(tags[:, r, :, :].bitcast(i32), xe[:, r, :, ID:ROW].bitcast(i32))
                ins.then_inc(s_tags, 1)
                dve.wait_ge(s_tags, it * 2 + r + 1)

            transposed(0, 0)
            keep_tags(0, 0)
            with dve.Fori(0, NP // 2 - 1) as it:
                transposed(it, 1)
                results(it, 0)
                results(it, 1)
                keep_tags(it, 1)
                transposed(it + 1, 0)
                results(it, 2)
                results(it, 3)
                keep_tags(it + 1, 0)
            it = NP // 2 - 1
            transposed(it, 1)
            results(it, 0)
            results(it, 1)
            keep_tags(it, 1)
            results(it, 2)
            results(it, 3)

            then_wait(nc.vector.tensor_tensor(acc[:], acc[:], rows[:, :, 0, 0:P], ALU.add))
            then_wait(nc.vector.tensor_tensor(acc[:], acc[:], ldb[:].unsqueeze(1).to_broadcast([P, NT, P]), ALU.add))
            for c in range(NC):
                a = acc[:, c * TC:(c + 1) * TC, :]
                dve.wait_ge(s_res[c], 16)
                then_wait(nc.vector.tensor_tensor(a, a, back[:, c * TC:(c + 1) * TC, 0:P], ALU.add))
                nc.vector.tensor_tensor(a, a, back[:, c * TC:(c + 1) * TC, P:2 * P], ALU.add).then_inc(s_acc, 1)

        @block.tensor
        def _(pe):
            mm = nc.tensor.matmul

            def transpose_chunk(c):
                for i in range(TC):
                    j = c * TC + i
                    pe.wait_ge(s_xn, j + 1)
                    last = nc.tensor.transpose(ps[:, GATE[c], i * P:(i + 1) * P], rows[:, j, 0, 0:P], ident[:])
                last.then_inc(s_xnt_ps, 1)

            def logits_chunk(c):
                pe.wait_ge(s_xnt, c + 1)
                for j in range(c * TC, (c + 1) * TC):
                    last = mm(logit_ps[c // 2][:, j % HT, :], xn_t[:, j * P:(j + 1) * P], wgate[:], start=True, stop=True,
                              skip_group_check=True)
                if c % 2:
                    last.then_inc(s_logits, 1)

            def projections(c):
                pe.wait_ge(s_xg, c + 1)
                if c:
                    pe.wait_ge(s_pj, 2 * c)
                for d in range(2):
                    mm(bank(PROJ[d]), watt[:, W_X + d, :], xg_t[:, chunk(c)], start=True, stop=True).then_inc(s_pj_ps, 1)

            def gates(c):
                if c:
                    pe.wait_ge(s_gate, 4 * c)
                for d in range(2):
                    pe.wait_ge(s_pj, 2 * c + d + 1)
                    for n, w in enumerate((W_GX, W_GA)):
                        mm(bank(GATE[2 * d + n]), watt[:, w + d, :], proj[:, d, chunk(c)],
                           start=True, stop=True).then_inc(s_gate_ps, 1)

            def ranks(h):
                pe.wait_ge(s_mask, h + 1)
                end = (h + 1) * HT
                mm(rank_ps[h], ones[0:1, :], slot_base[:], start=True, stop=False)
                mm(rank_ps[h], before[:], mask[:, half(h), :], start=False, stop=False)
                for j in range(end - 1):
                    to = slice(max(j + 1 - h * HT, 0), HT)
                    last = mm(rank_ps[h][:, to, :], ones[:], mask[:, j:j + 1, :].to_broadcast([P, HT - to.start, E]),
                              start=False, stop=(j == end - 2))
                last.then_inc(s_rank, 1)

            pe.wait_ge(s_cst, 6)
            pe.wait_ge(s_wgate, 16)
            transpose_chunk(0)
            transpose_chunk(1)
            for c in range(NC):
                logits_chunk(c)
                if c + 2 < NC:
                    transpose_chunk(c + 2)
            ranks(0)
            pe.wait_ge(s_wts, 48)
            projections(0)
            gates(0)
            ranks(1)
            projections(1)
            for c in range(1, NC):
                gates(c)
                if c + 1 < NC:
                    projections(c + 1)

            def outputs(c):
                pe.wait_ge(s_h, c + 1)
                if c >= 2:
                    pe.wait_ge(s_z, c - 1)
                else:
                    pe.wait_ge(s_pj, 2 * NC)
                mm(bank(PROJ[c % 2]), watt[:, W_O, :], gate_x[:, 0, chunk(c)], start=True, stop=False)
                mm(bank(PROJ[c % 2]), watt[:, W_O + 1, :], gate_x[:, 1, chunk(c)], start=False, stop=True).then_inc(s_o_ps, 1)

            def last_projection(c):
                pe.wait_ge(s_g, c + 1)
                if c >= 2:
                    pe.wait_ge(s_ld, c - 1)
                else:
                    pe.wait_ge(s_slot, 2)
                for i in range(TC):
                    j = c * TC + i
                    last = mm(ps[:, ROUTE[c % 2], i * P:(i + 1) * P], xg_t[:, j * P:(j + 1) * P], watt[:, W_LD, :],
                              start=True, stop=True, skip_group_check=True)
                last.then_inc(s_ld_ps, 1)

            outputs(0)
            outputs(1)
            outputs(2)
            last_projection(0)
            last_projection(1)
            outputs(3)
            last_projection(2)
            last_projection(3)

            pe.sem_inc(s_up, 4)
            pe.sem_inc(s_down, 2)
            pe.wait_ge(s_gate, 4 * NC)
            pe.wait_ge(s_z, NC)
            pe.wait_ge(s_ld, NC)

            def transpose_rows(it, r):
                pe.wait_ge(s_xe[r], it * 16 + 16)
                pe.wait_ge(s_xet, it * 2 + r + 1)
                for n in range(PT):
                    last = nc.tensor.transpose(xet_ps[:, n * P:(n + 1) * P], xe[:, r, n, 0:P], ident[:])
                last.then_inc(s_xet_ps, 1)

            def up(it, s):
                r, o = s // 2, s % 2
                if o == 0:
                    pe.wait_ge(s_xet, it * 2 + r + 2)
                    pe.wait_ge(s_wexp[r], it * 32 + 32)
                pe.wait_ge(s_gelu, it * 4 + s + 1)
                for b in range(FB):
                    last = mm(ps[:, HID[o] + b, 0:CAP], w1[:, r, o, b * P:(b + 1) * P],
                              xe_t[:, r, o * CAP:(o + 1) * CAP], start=True, stop=True)
                last.then_inc(s_up, 1)

            def down(it, s):
                r, o = s // 2, s % 2
                pe.wait_ge(s_gelu, it * 4 + s + 3)
                pe.wait_ge(s_y, it * 4 + s + 1)
                for n in range(3):
                    for b in range(FB):
                        last = mm(ps[:, RES[o], n * P:(n + 1) * P], hid[:, o, b, n * P:(n + 1) * P],
                                  w2[:, r, o, b, :], start=(b == 0), stop=(b == FB - 1))
                last.then_inc(s_down, 1)

            transpose_rows(0, 0)
            up(0, 0)
            with pe.Fori(0, NP // 2 - 1) as it:
                transpose_rows(it, 1)
                up(it, 1)
                down(it, 0)
                up(it, 2)
                down(it, 1)
                transpose_rows(it + 1, 0)
                up(it, 3)
                down(it, 2)
                up(it + 1, 0)
                down(it, 3)
            it = NP // 2 - 1
            transpose_rows(it, 1)
            up(it, 1)
            down(it, 0)
            up(it, 2)
            down(it, 1)
            up(it, 3)
            down(it, 2)
            down(it, 3)


def kernel(**inputs):
    import numpy as np
    import concourse.bacc as bacc
    from concourse.bass_utils import run_bass_kernel_spmd

    fp32 = mybir.dt.float32
    a = {k: np.asarray(v) for k, v in inputs.items()}
    att = {k[len("L0_attn_"):]: v for k, v in a.items() if k.startswith("L0_attn_")}
    both = [f"{d}_{n}" for n in ("Wx", "Wgx", "Wga", "Wo") for d in ("fwd", "bwd")]
    cols = [f"{d}_{n}" for n in ("a_logit", "bx", "bgx", "bga", "bo") for d in ("fwd", "bwd")]
    x = att["x"]
    arrays = {
        "x_d": x.reshape(16, 128, 128).transpose(1, 0, 2).reshape(128, 2048),
        "w_att_d": np.concatenate([att[n] for n in both] + [att["ld_W"]], axis=1),
        "w_gate_d": a["L0_ffn_gate_w"].T,
        "cols_d": np.stack([att[n] for n in cols], axis=1),
        "ldb_d": att["ld_b"].reshape(128),
        "w1_d": a["L0_ffn_w1"],
        "w2_d": a["L0_ffn_w2"].reshape(16, 2, 128, 128).transpose(0, 2, 1, 3).reshape(16, 128, 256),
    }
    arrays = {k: np.ascontiguousarray(v) for k, v in arrays.items()}
    nc = bacc.Bacc("TRN2", target_bir_lowering=False, num_devices=1)
    aps = [nc.dram_tensor(k, v.shape, fp32, kind="ExternalInput").ap() for k, v in arrays.items()]
    out = nc.dram_tensor("out_d", (128, 2048), fp32, kind="ExternalOutput").ap()
    rglru_moe(nc, *aps, out)
    r = run_bass_kernel_spmd(nc, [arrays], core_ids=[0])
    y = r.results[0]["out_d"]
    return y.reshape(128, 16, 128).transpose(1, 0, 2).reshape(x.shape)
```

```python
from contextlib import ExitStack

import concourse.bass as bass
from concourse import mybir


def rglru_moe(nc, x_in, w_att, w_gate, cols_in, ldb_in, w1_in, w2_in, y_out):
    fp32 = mybir.dt.float32
    bf16 = mybir.dt.bfloat16
    i32 = mybir.dt.int32
    ALU = mybir.AluOpType
    ACT = mybir.ActivationFunctionType
    AX = mybir.AxisListType

    P = 128
    T = 2048
    SEQ = 256
    NT = T // P
    TC = 4
    NC = NT // TC
    GROUPS = [(0, 4), (4, 12), (12, 16)]
    PIECES = [(0, 2), (2, 6), (6, 10), (10, 14), (14, 16)]
    POOL_PIECE = 2
    GT = max(end - start for start, end in GROUPS)
    CW = TC * P
    E = 16
    K = 2
    F = 256
    FB = F // P
    CAP = int(1.25 * T * K / E)
    NSLOT = E * CAP
    ROW = P + 1
    ID = P
    PT = 2 * CAP // P
    HALF = CAP - 2 * P
    NP = E // 2
    EPS = 1e-5
    W_EPS = 1e-6
    SAT = 17.5
    DROP = 8192.0
    ER = 4
    NO_ID = 1 << 20
    OUT_OF_RACE = -1e30
    (A_LOGIT, B_X, B_GX, B_GA, B_O) = range(0, 10, 2)
    (W_X, W_GX, W_GA, W_O) = range(0, 8, 2)
    W_LD = 8

    slot_rows = nc.dram_tensor("slot_rows", [NSLOT, ROW], fp32, kind="Internal").ap()
    choice_rows = nc.dram_tensor("choice_rows", [T * K, P], fp32, kind="Internal").ap()

    ctx = ExitStack()
    with ctx:
        def sb(name, shape, dt=fp32):
            return ctx.enter_context(nc.sbuf_tensor(name, shape, dt))

        def sem(name):
            return ctx.enter_context(nc.semaphore(name))

        x = sb("x", [P, NT, P])
        rows = sb("rows", [P, NT, K, ROW])
        acc = sb("acc", [P, NT, P])
        xn_t = sb("xn_t", [P, T])
        xg_t = sb("xg_t", [P, T])
        proj = sb("proj", [P, 2, T])
        gate_x = sb("gate_x", [P, 2, T])
        decay = sb("decay", [P, 2, T])
        norm = sb("norm", [P, 2, T])
        watt = sb("watt", [P, 9, P])
        wgate = sb("wgate", [P, E])
        cols = sb("cols", [P, 10])
        ldb = sb("ldb", [P, P])
        consts = sb("consts", [P, 2])
        unused = sb("unused", [P, 8])
        aexp = sb("aexp", [P, 2])
        bo_half = sb("bo_half", [P, 1])
        ident = sb("ident", [P, P])
        twice = sb("twice", [P, P])
        before = sb("before", [P, P], bf16)
        ones = sb("ones", [P, P], bf16)
        first_key = sb("first_key", [P, E])
        slot_base = sb("slot_base", [1, GT, E], bf16)
        slot_end = sb("slot_end", [P, E])
        stats = sb("stats", [P, NT, 6])
        mv = sb("mv", [P, NT, 2])
        std = sb("std", [P, NT])
        rstd = sb("rstd", [P, NT])
        shift = sb("shift", [P, NT])
        logit = sb("logit", [P, NT, E])
        logit2 = sb("logit2", [P, NT, E])
        best = sb("best", [P, K, NT])
        hit = sb("hit", [P, GT, E])
        key = sb("key", [P, GT])
        chosen = sb("chosen", [P, K, NT, E])
        mask = sb("mask", [P, NT, E], bf16)
        over = sb("over", [P, GT, E])
        slot_e = sb("slot_e", [P, GT, E])
        slot_k = sb("slot_k", [P, K, GT, E])
        slot = sb("slot", [P, K, NT], i32)
        prob = sb("prob", [P, K, NT])
        prob_sum = sb("prob_sum", [P, NT])
        weight = sb("weight", [P, K, NT])
        empty_rows = sb("empty_rows", [P, ER, ROW])
        zeros = sb("zeros", [P, 8 * P])
        w1 = sb("w1", [P, 2, 2, F])
        w2 = sb("w2", [P, 2, 2, FB, P])
        xe = sb("xe", [P, 2, PT, ROW])
        tags = sb("tags", [P, 2, PT], i32)
        xe_t = sb("xe_t", [P, 2, PT * P])
        hid = sb("hid", [P, 2, FB, 3 * P])
        ye = sb("ye", [P, 2, PT, P])
        back = sb("back", [P, NT, K * P])

        ps = ctx.enter_context(nc.psum_tensor("ps", [P, 8, 512], fp32))

        s_x = [sem(f"s_x{c}") for c in range(NC)]
        s_wts = sem("s_wts")
        s_wgate = sem("s_wgate")
        s_tags = sem("s_tags")
        s_tags_free = sem("s_tags_free")
        s_empty = sem("s_empty")
        s_slots_empty = sem("s_slots_empty")
        s_zeroed = sem("s_zeroed")
        s_shift = sem("s_shift")
        s_cst = sem("s_cst")
        s_dcst = sem("s_dcst")
        s_pool = sem("s_pool")
        s_dve = sem("s_dve")
        s_var = sem("s_var")
        s_std = sem("s_std")
        s_rstd = sem("s_rstd")
        s_xn = [sem(f"s_xn{c}") for c in range(NC)]
        s_xnt_ps = sem("s_xnt_ps")
        s_xnt = sem("s_xnt")
        s_xg = sem("s_xg")
        s_logits = sem("s_logits")
        s_mask = sem("s_mask")
        s_rank = sem("s_rank")
        s_best = sem("s_best")
        s_prob = sem("s_prob")
        s_aexp = sem("s_aexp")
        s_rows2 = sem("s_rows2")
        s_id = sem("s_id")
        s_weight = sem("s_weight")
        s_slot = sem("s_slot")
        s_sent = sem("s_sent")
        s_pj_ps = sem("s_pj_ps")
        s_pj = sem("s_pj")
        s_gate_ps = sem("s_gate_ps")
        s_gate = sem("s_gate")
        s_a = sem("s_a")
        s_sq = sem("s_sq")
        s_norm = sem("s_norm")
        s_in = sem("s_in")
        s_h = sem("s_h")
        s_o_ps = sem("s_o_ps")
        s_g = sem("s_g")
        s_ld_ps = sem("s_ld_ps")
        s_ld = sem("s_ld")
        s_w1 = [sem(f"s_w1{r}") for r in range(2)]
        s_w2 = [sem(f"s_w2{r}") for r in range(2)]
        s_xe = [sem(f"s_xe{r}") for r in range(2)]
        s_xet_ps = sem("s_xet_ps")
        s_xet = sem("s_xet")
        s_up = sem("s_up")
        s_gelu = sem("s_gelu")
        s_down = sem("s_down")
        s_y = sem("s_y")
        s_turn = sem("s_turn")
        s_back = [sem(f"s_back{r}") for r in range(2)]
        s_res = [sem(f"s_res{n}") for n in range(len(PIECES))]
        s_second = sem("s_second")
        s_acc = [sem(f"s_acc{n}") for n in range(len(PIECES))]
        s_first = sem("s_first")
        s_out = sem("s_out")

        x_ap = x_in.rearrange("p (j d) -> p j d", d=P)
        out_ap = y_out.rearrange("p (j d) -> p j d", d=P)
        choice_ap = choice_rows.rearrange("(j p k) d -> p j (k d)", p=P, k=K)

        def bank(b, n=512):
            return ps[:, b, 0:n]

        def chunk(c):
            return slice(c * CW, (c + 1) * CW)

        GATE = [0, 1, 2, 3]
        PROJ = [4, 5]
        ROUTE = [6, 7]
        OUT = [0, 1, 4, 5]
        LD = [2, 3, 6, 7]

        def route_ps(g, part):
            n = (GROUPS[g][1] - GROUPS[g][0]) * E
            return ps[:, ROUTE[g % 2], part * n:(part + 1) * n].rearrange("p (j e) -> p j e", e=E)

        logit_ps = [route_ps(g, 0) for g in range(len(GROUPS))]
        rank_ps = [route_ps(g, 1) for g in range(len(GROUPS))]
        XE_T, HID, RES = 0, [2, 4], [6, 7]
        xet_ps = ps[:, XE_T:XE_T + 2, :].rearrange("p b n -> p (b n)")[:, 0:PT * P]

        block = ctx.enter_context(nc.Block())

        @block.sync
        def _(sp):
            for c in (0, 2, 3):
                sp.dma_start(x[:, c * TC:(c + 1) * TC, :], x_ap[:, c * TC:(c + 1) * TC, :]).then_inc(s_x[c], 16)
            sp.dma_start(wgate[:], w_gate).then_inc(s_wgate, 16)
            sp.wait_ge(s_empty, 2)
            sp.dma_start(slot_rows.rearrange("(p a n) r -> p a (n r)", p=P, n=ER),
                         empty_rows[:].rearrange("p n r -> p (n r)").unsqueeze(1).to_broadcast(
                             [P, NSLOT // P // ER, ER * ROW])).then_inc(s_slots_empty, 16)
            sp.dma_start(watt[:], w_att.rearrange("d (n f) -> d n f", f=P)).then_inc(s_wts, 16)
            sp.dma_start(cols[:], cols_in).then_inc(s_wts, 16)
            sp.dma_start(ldb[:], ldb_in.partition_broadcast(P)).then_inc(s_wts, 16)
            sp.wait_ge(s_dcst, 2)
            sp.dma_start(choice_rows.rearrange("(p a n) d -> p a (n d)", p=P, n=8),
                         zeros[:].unsqueeze(1).to_broadcast([P, T * K // P // 8, 8 * P])).then_inc(s_zeroed, 16)

            def load_rows(it, r):
                q = it * 2 + r
                sp.dma_start(xe[:, r, :, :], slot_rows[bass.ds(q * (PT * P), PT * P), :].rearrange(
                    "(n p) r -> p n r", p=P)).then_inc(s_xe[r], 16)

            sp.wait_ge(s_sent, 16 * NT * K)
            for r in range(2):
                load_rows(0, r)
            sp.sem_inc(s_tags_free, 2)
            sp.wait_ge(s_tags, 1)
            load_rows(1, 0)

            def refill(it, r):
                sp.wait_ge(s_tags, it * 2 + r)
                load_rows(it + r, 1 - r)

            def free_tags(it, r):
                sp.wait_ge(s_back[r], it * (16 * PT))
                sp.sem_inc(s_tags_free, 1)

            with sp.Fori(1, NP // 2 - 1) as it:
                for r in range(2):
                    refill(it, r)
                    free_tags(it, r)
            refill(NP // 2 - 1, 0)
            free_tags(NP // 2 - 1, 0)
            free_tags(NP // 2 - 1, 1)
            for r in range(2):
                sp.wait_ge(s_back[r], 16 * PT * (NP // 2))
            for n, (start, end) in enumerate(PIECES):
                sp.dma_start(back[:, start:end, :], choice_ap[:, start:end, :]).then_inc(s_res[n], 16)
            for n, (start, end) in enumerate(PIECES):
                if n == POOL_PIECE:
                    continue
                sp.wait_ge(s_acc[n], 1)
                sp.dma_start(out_ap[:, start:end, :], acc[:, start:end, :]).then_inc(s_out, 16)
            sp.wait_ge(s_out, 16 * len(PIECES))

        @block.gpsimd
        def _(pool):
            steps = [0]

            def then_wait(ins):
                steps[0] += 1
                ins.then_inc(s_pool, 1)
                pool.wait_ge(s_pool, steps[0])

            nc.gpsimd.memset(empty_rows[:, :, 0:ID], 0.0).then_inc(s_empty, 1)
            nc.gpsimd.memset(empty_rows[:, :, ID:ROW].bitcast(i32), NO_ID).then_inc(s_empty, 1)
            then_wait(nc.gpsimd.memset(ident[:], 0.0))
            nc.gpsimd.affine_select(out=ident[:], in_=ident[:], compare_op=ALU.not_equal, fill=1.0, base=0,
                                    pattern=[[-1, P]], channel_multiplier=1).then_inc(s_cst, 1)
            then_wait(nc.gpsimd.memset(before[:], 0.0))
            nc.gpsimd.affine_select(out=before[:], in_=before[:], compare_op=ALU.is_ge, fill=1.0, base=0,
                                    pattern=[[-1, P]], channel_multiplier=1).then_inc(s_cst, 1)
            nc.gpsimd.iota(first_key[:], pattern=[[-1, E]], base=E, channel_multiplier=0,
                           allow_small_or_imprecise_dtypes=True).then_inc(s_cst, 1)
            nc.gpsimd.iota(slot_base[:], pattern=[[0, GT], [CAP, E]], base=0, channel_multiplier=0,
                           allow_small_or_imprecise_dtypes=True).then_inc(s_cst, 1)
            nc.gpsimd.iota(slot_end[:], pattern=[[CAP, E]], base=CAP, channel_multiplier=0,
                           allow_small_or_imprecise_dtypes=True).then_inc(s_cst, 1)
            nc.gpsimd.memset(ones[:], 1.0).then_inc(s_cst, 1)
            then_wait(nc.gpsimd.memset(twice[:], 0.0))
            nc.gpsimd.affine_select(out=twice[:], in_=twice[:], compare_op=ALU.not_equal, fill=2.0, base=0,
                                    pattern=[[-1, P]], channel_multiplier=1).then_inc(s_cst, 1)
            for k in range(K):
                nc.gpsimd.iota(rows[:, :, k, ID:ROW].bitcast(i32), pattern=[[P * K, NT], [0, 1]], base=k,
                               channel_multiplier=K).then_inc(s_id, 1)

            def copy_rows(c):
                pool.wait_ge(s_xn[c], TC)
                nc.gpsimd.tensor_copy(rows[:, c * TC:(c + 1) * TC, 1, 0:P],
                                      rows[:, c * TC:(c + 1) * TC, 0, 0:P]).then_inc(s_rows2, 1)

            for c in range(NC - 1):
                copy_rows(c)
            pool.wait_ge(s_id, K)
            pool.wait_ge(s_slots_empty, 16)
            for g, (start, end) in enumerate(GROUPS):
                pool.wait_ge(s_slot, g + 1)
                pool.wait_ge(s_rows2, end // TC)
                for j in range(start, end):
                    for k in range(K):
                        pool.indirect_dma_start(slot_rows, bass.IndirectOffsetOnAxis(slot[:, k, j:j + 1], 0),
                                                rows[:, j, k, :], None, bounds_check=NSLOT - 1,
                                                oob_is_err=False).then_inc(s_sent, 16)

            last_id = pool.to_reg(T * K - 1)
            pool.wait_ge(s_zeroed, 16)
            with pool.Fori(0, NP // 2) as it:
                for r in range(2):
                    for n in range(PT):
                        if n in (0, 2):
                            pool.wait_ge(s_y, it * 4 + 2 * r + (3 if n == 0 else 4))
                            pool.sem_inc(s_turn, 1)
                        pool.indirect_dma_start(
                            choice_rows, bass.IndirectOffsetOnAxis(tags[:, r, n:n + 1], 0),
                            ye[:, r, n, :], None, bounds_check=last_id, oob_is_err=False).then_inc(s_back[r], 16)

            start, end = PIECES[POOL_PIECE]
            pool.wait_ge(s_first, 1)
            pool.wait_ge(s_second, POOL_PIECE + 1)
            nc.gpsimd.tensor_tensor(acc[:, start:end, :], acc[:, start:end, :], back[:, start:end, P:2 * P],
                                    ALU.add).then_inc(s_acc[POOL_PIECE], 1)

        @block.scalar
        def _(act):
            act.dma_start(x[:, TC:2 * TC, :], x_ap[:, TC:2 * TC, :]).then_inc(s_x[1], 16)

            def load_w1(it, r):
                act.dma_start(w1[:, r, :, :], w1_in[bass.ds((it * 2 + r) * 2, 2), :, :].rearrange(
                    "e d f -> d e f")).then_inc(s_w1[r], 16)

            def load_w2(it, r):
                act.dma_start(w2[:, r, :, :, :].rearrange("p a b d -> p a (b d)"),
                              w2_in[bass.ds((it * 2 + r) * 2, 2), :, :].rearrange("e p n -> p e n")).then_inc(s_w2[r], 16)

            tables = [0]

            def load_table(func):
                nc.scalar.activation(unused[:, tables[0]:tables[0] + 1], consts[:, 1:2], func)
                tables[0] += 1

            def root(c):
                act.wait_ge(s_var, c + 1)
                nc.scalar.activation(std[:, c * TC:(c + 1) * TC], mv[:, c * TC:(c + 1) * TC, 1], ACT.Sqrt,
                                     bias=consts[:, 0:1]).then_inc(s_std, 1)

            def copy_out(c):
                act.wait_ge(s_xnt_ps, c + 1)
                nc.scalar.copy(xn_t[:, chunk(c)], bank(GATE[c])).then_inc(s_xnt, 1)

            def gelu_in(c):
                act.wait_ge(s_xnt, c + 1)
                nc.scalar.activation(xg_t[:, chunk(c)], xn_t[:, chunk(c)], ACT.Gelu_apprx_tanh).then_inc(s_xg, 1)

            def project(c):
                for d in range(2):
                    act.wait_ge(s_pj_ps, 2 * c + d + 1)
                    nc.scalar.activation(proj[:, d, chunk(c)], bank(PROJ[d]), ACT.Identity,
                                         bias=cols[:, B_X + d:B_X + d + 1]).then_inc(s_pj, 1)

            def normalise(c):
                act.wait_ge(s_shift, c - 1)
                act.wait_ge(s_x[c], 16)
                for j in range(c * TC, (c + 1) * TC):
                    nc.scalar.activation(rows[:, j, 0, 0:P], x[:, j, :], ACT.Identity, scale=rstd[:, j:j + 1],
                                         bias=shift[:, j:j + 1]).then_inc(s_xn[c], 1)

            act.wait_ge(s_dcst, 1)
            load_table(ACT.Sqrt)
            root(0)
            root(1)
            copy_out(0)
            root(2)
            root(3)
            normalise(2)
            copy_out(1)
            normalise(3)
            copy_out(2)
            copy_out(3)
            load_table(ACT.Gelu_apprx_tanh)
            gelu_in(0)
            gelu_in(1)
            gelu_in(2)
            gelu_in(3)
            act.wait_ge(s_wts, 48)
            project(0)
            load_table(ACT.Sigmoid)
            project(1)
            act.wait_ge(s_rows2, NC - 1)
            act.wait_ge(s_xn[NC - 1], TC)
            nc.scalar.copy(rows[:, (NC - 1) * TC:, 1, 0:P], rows[:, (NC - 1) * TC:, 0, 0:P]).then_inc(s_rows2, 1)
            nc.scalar.activation(aexp[:], cols[:, A_LOGIT:A_LOGIT + 2], ACT.Sigmoid).then_inc(s_aexp, 1)
            load_w1(0, 0)
            load_w1(0, 1)
            load_w2(0, 0)

            def gates(c):
                for d in range(2):
                    for n, (dst, b) in enumerate(((gate_x, B_GX), (decay, B_GA))):
                        act.wait_ge(s_gate_ps, 4 * c + 2 * d + n + 1)
                        nc.scalar.activation(dst[:, d, chunk(c)], bank(GATE[2 * d + n]), ACT.Sigmoid,
                                             bias=cols[:, b + d:b + d + 1]).then_inc(s_gate, 1)

            def square(c):
                act.wait_ge(s_a, c + 1)
                nc.scalar.activation(norm[:, :, chunk(c)], decay[:, :, chunk(c)], ACT.Square).then_inc(s_sq, 1)

            def norms(c):
                act.wait_ge(s_sq, c + 1)
                for ds in ((slice(0, 1), slice(1, 2)) if c == 0 else (slice(0, 2),)):
                    nc.scalar.activation(norm[:, ds, chunk(c)], norm[:, ds, chunk(c)], ACT.Sqrt,
                                         scale=-1.0, bias=consts[:, 1:2]).then_inc(s_norm, 1)

            gates(0)
            act.wait_ge(s_best, K * len(GROUPS))
            nc.scalar.activation(prob[:], best[:], ACT.Sigmoid).then_inc(s_prob, 1)
            project(2)
            gates(1)
            project(3)
            gates(2)
            gates(3)
            norms(0)
            norms(1)
            norms(2)
            square(3)
            norms(3)
            load_table(ACT.Gelu_apprx_tanh)
            for c in range(NC):
                act.wait_ge(s_o_ps, c + 1)
                nc.scalar.activation(xg_t[:, chunk(c)], bank(OUT[c]), ACT.Gelu_apprx_tanh,
                                     scale=0.5, bias=bo_half[:]).then_inc(s_g, 1)
            load_table(ACT.Gelu)
            act.sem_inc(s_gelu, 2)
            act.wait_ge(s_dcst, 2)

            def expert(it, s):
                o = s % 2
                act.wait_ge(s_up, it * 4 + s + 5)
                act.wait_ge(s_down, it * 4 + s + 1)
                nc.scalar.activation(hid[:, o, :, o * HALF:o * HALF + CAP],
                                     ps[:, HID[o]:HID[o] + FB, 0:CAP], ACT.Gelu).then_inc(s_gelu, 1)

            with act.Fori(0, NP // 2 - 1) as it:
                expert(it, 0)
                expert(it, 1)
                load_w1(it + 1, 0)
                load_w2(it, 1)
                expert(it, 2)
                expert(it, 3)
                load_w1(it + 1, 1)
                load_w2(it + 1, 0)
            it = NP // 2 - 1
            expert(it, 0)
            expert(it, 1)
            load_w2(it, 1)
            expert(it, 2)
            expert(it, 3)

            act.wait_ge(s_weight, 1)
            for n, (start, end) in enumerate(PIECES):
                act.wait_ge(s_res[n], 16)
                for j in range(start, end):
                    last = nc.scalar.activation(back[:, j, P:2 * P], back[:, j, P:2 * P], ACT.Copy,
                                                scale=weight[:, 1, j:j + 1])
                last.then_inc(s_second, 1)
            start, end = PIECES[POOL_PIECE]
            act.wait_ge(s_acc[POOL_PIECE], 1)
            act.dma_start(out_ap[:, start:end, :], acc[:, start:end, :]).then_inc(s_out, 16)

        @block.vector
        def _(dve):
            steps = [0]

            def then_wait(ins):
                steps[0] += 1
                ins.then_inc(s_dve, 1)
                dve.wait_ge(s_dve, steps[0])

            nc.vector.memset(consts[:, 0:1], EPS)
            nc.vector.memset(consts[:, 1:2], 1.0).then_inc(s_dcst, 1)
            nc.vector.memset(zeros[:], 0.0)
            nc.vector.memset(hid[:, 0, :, CAP:3 * P], 0.0)
            nc.vector.memset(hid[:, 1, :, 0:HALF], 0.0).then_inc(s_dcst, 1)

            def moments(c):
                dve.wait_ge(s_x[c], 16)
                for j in range(c * TC, (c + 1) * TC):
                    last = nc.vector.bn_stats(stats[:, j, :], x[:, j, :])
                then_wait(last)
                for j in range(c * TC, (c + 1) * TC):
                    last = nc.vector.bn_aggr(mv[:, j, :], stats[:, j, :])
                last.then_inc(s_var, 1)

            def deviations(c):
                dve.wait_ge(s_std, c + 1)
                nc.vector.reciprocal(rstd[:, c * TC:(c + 1) * TC], std[:, c * TC:(c + 1) * TC]).then_inc(s_rstd, 1)

            def normalise(c):
                dve.wait_ge(s_rstd, c + 1)
                for j in range(c * TC, (c + 1) * TC):
                    nc.vector.tensor_scalar(rows[:, j, 0, 0:P], x[:, j, :], mv[:, j, 0:1], rstd[:, j:j + 1],
                                            ALU.subtract, ALU.mult).then_inc(s_xn[c], 1)

            def shifts(c):
                dve.wait_ge(s_rstd, c + 1)
                js = slice(c * TC, (c + 1) * TC)
                nc.vector.scalar_tensor_tensor(shift[:, js], mv[:, js, 0], -1.0, rstd[:, js],
                                               ALU.mult, ALU.mult).then_inc(s_shift, 1)

            moments(0)
            moments(1)
            deviations(0)
            normalise(0)
            moments(2)
            deviations(1)
            moments(3)
            deviations(2)
            shifts(2)
            normalise(1)
            deviations(3)
            shifts(3)

            def choose(g):
                js = slice(*GROUPS[g])
                n = js.stop - js.start
                shape = [P, n, E]
                keys = first_key[:].unsqueeze(1).to_broadcast(shape)
                dve.wait_ge(s_logits, g + 1)
                then_wait(nc.vector.tensor_scalar(logit[:, js, :], logit_ps[g], SAT, None, ALU.min))
                for k, src in enumerate((logit, logit2)):
                    nc.vector.tensor_reduce(best[:, k, js], src[:, js, :], AX.X, ALU.max).then_inc(s_best, 1)
                    dve.wait_ge(s_best, 2 * g + k + 1)
                    then_wait(nc.vector.tensor_tensor(hit[:, 0:n, :], src[:, js, :],
                                                      best[:, k, js].unsqueeze(2).to_broadcast(shape), ALU.is_equal))
                    then_wait(nc.vector.tensor_tensor(hit[:, 0:n, :], hit[:, 0:n, :], keys, ALU.mult))
                    then_wait(nc.vector.tensor_reduce(key[:, 0:n], hit[:, 0:n, :], AX.X, ALU.max))
                    then_wait(nc.vector.tensor_tensor(chosen[:, k, js, :], keys,
                                                      key[:, 0:n].unsqueeze(2).to_broadcast(shape), ALU.is_equal))
                    if k == 0:
                        then_wait(nc.vector.scalar_tensor_tensor(logit2[:, js, :], chosen[:, 0, js, :], OUT_OF_RACE,
                                                                 logit[:, js, :], ALU.mult, ALU.add))
                nc.vector.tensor_tensor(mask[:, js, :], chosen[:, 0, js, :], chosen[:, 1, js, :],
                                        ALU.add).then_inc(s_mask, 1)

            def place(g):
                js = slice(*GROUPS[g])
                n = js.stop - js.start
                dve.wait_ge(s_rank, g + 1)
                then_wait(nc.vector.tensor_tensor(over[:, 0:n, :], rank_ps[g],
                                                  slot_end[:].unsqueeze(1).to_broadcast([P, n, E]), ALU.is_ge))
                then_wait(nc.vector.scalar_tensor_tensor(slot_e[:, 0:n, :], over[:, 0:n, :], DROP, rank_ps[g],
                                                         ALU.mult, ALU.add))
                then_wait(nc.vector.tensor_tensor(slot_k[:, :, 0:n, :], chosen[:, :, js, :],
                                                  slot_e[:, 0:n, :].unsqueeze(1).to_broadcast([P, K, n, E]), ALU.mult))
                with nc.allow_low_precision("one whole number below 2^24 and zeros are added"):
                    nc.vector.tensor_reduce(slot[:, :, js], slot_k[:, :, 0:n, :], AX.X, ALU.add).then_inc(s_slot, 1)

            dve.wait_ge(s_cst, 6)
            choose(0)
            place(0)
            choose(1)
            place(1)
            choose(2)

            dve.wait_ge(s_aexp, 1)
            then_wait(nc.vector.tensor_tensor(bo_half[:], cols[:, B_O:B_O + 1], cols[:, B_O + 1:B_O + 2], ALU.add))
            then_wait(nc.vector.tensor_scalar(bo_half[:], bo_half[:], 0.5, None, ALU.mult))

            def decays(c):
                dve.wait_ge(s_gate, 4 * (c + 1))
                for d in range(2):
                    last = nc.vector.tensor_scalar(decay[:, d, chunk(c)], decay[:, d, chunk(c)], aexp[:, d:d + 1], 1.0,
                                                   ALU.mult, ALU.min)
                last.then_inc(s_a, 1)
                if c < NC - 1:
                    dve.wait_ge(s_a, c + 1)
                    nc.vector.tensor_tensor(norm[:, :, chunk(c)], decay[:, :, chunk(c)], decay[:, :, chunk(c)],
                                            ALU.mult).then_inc(s_sq, 1)
                nc.vector.tensor_tensor(gate_x[:, :, chunk(c)], gate_x[:, :, chunk(c)], proj[:, :, chunk(c)], ALU.mult)

            decays(0)
            place(2)
            decays(1)
            dve.wait_ge(s_prob, 1)
            then_wait(nc.vector.scalar_tensor_tensor(prob_sum[:], prob[:, 0, :], W_EPS, prob[:, 1, :], ALU.add, ALU.add))
            then_wait(nc.vector.reciprocal(prob_sum[:], prob_sum[:]))
            nc.vector.tensor_tensor(weight[:], prob[:], prob_sum[:].unsqueeze(1).to_broadcast([P, K, NT]),
                                    ALU.mult).then_inc(s_weight, 1)
            decays(2)
            decays(3)

            def scan(c):
                lo, hi = c * CW, (c + 1) * CW
                for d in range(2):
                    edge = 0 if d == 0 else SEQ - 1
                    dve.wait_ge(s_norm, d + 1 if c == 0 else c + 2)
                    nc.vector.memset(decay[:, d, chunk(c)].rearrange("p (n s) -> p n s", s=SEQ)[:, :, edge], 0.0)
                    nc.vector.tensor_tensor(proj[:, d, chunk(c)], norm[:, d, chunk(c)], gate_x[:, d, chunk(c)],
                                            ALU.mult).then_inc(s_in, 1)
                rev = slice(hi - 1, lo - 1 if lo else None, -1)
                for d, way in enumerate((slice(lo, hi), rev)):
                    dve.wait_ge(s_in, 2 * c + d + 1)
                    nc.vector.tensor_tensor_scan(gate_x[:, d, way], decay[:, d, way], proj[:, d, way], 0.0,
                                                 ALU.mult, ALU.add).then_inc(s_h, 1)

            def add_ld(c):
                dve.wait_ge(s_ld_ps, c + 1)
                a = acc[:, c * TC:(c + 1) * TC, :].rearrange("p j d -> p (j d)")
                nc.vector.tensor_tensor(a, x[:, c * TC:(c + 1) * TC, :].rearrange("p j d -> p (j d)"),
                                        bank(LD[c]), ALU.add).then_inc(s_ld, 1)

            for c in range(NC):
                scan(c)
            add_ld(0)
            add_ld(1)

            dve.sem_inc(s_xet, 1)

            def transposed(it, r):
                dve.wait_ge(s_xet_ps, it * 2 + r + 1)
                dve.wait_ge(s_up, it * 4 + 2 * r + 2)
                nc.vector.tensor_copy(xe_t[:, r, :], xet_ps).then_inc(s_xet, 1)

            def results(it, s):
                r, o = s // 2, s % 2
                y_ps = bank(RES[o], 3 * P).rearrange("p (n d) -> p n d", d=P)
                dve.wait_ge(s_down, it * 4 + s + 3)
                full, part = (slice(0, 2), slice(2, 3)) if o == 0 else (slice(1, 3), slice(0, 1))
                tiles = slice(0, 2) if o == 0 else slice(3, 5)
                lanes = slice(0, HALF) if o == 0 else slice(HALF, P)
                nc.vector.tensor_copy(ye[:, r, tiles, :], y_ps[:, full, :])
                nc.vector.tensor_copy(ye[lanes, r, 2:3, :], y_ps[lanes, part, :]).then_inc(s_y, 1)

            def keep_tags(it, r):
                dve.wait_ge(s_tags_free, it * 2 + r + 1)
                ins = nc.vector.tensor_copy(tags[:, r, :], xe[:, r, :, ID].bitcast(i32))
                ins.then_inc(s_tags, 1)
                dve.wait_ge(s_tags, it * 2 + r + 1)

            transposed(0, 0)
            keep_tags(0, 0)
            add_ld(2)
            add_ld(3)
            dve.wait_ge(s_ld, NC)
            dve.sem_inc(s_y, 2)
            with dve.Fori(0, NP // 2 - 1) as it:
                transposed(it, 1)
                results(it, 0)
                results(it, 1)
                keep_tags(it, 1)
                transposed(it + 1, 0)
                results(it, 2)
                results(it, 3)
                keep_tags(it + 1, 0)
            it = NP // 2 - 1
            transposed(it, 1)
            results(it, 0)
            results(it, 1)
            keep_tags(it, 1)
            results(it, 2)
            results(it, 3)

            then_wait(nc.vector.tensor_tensor(acc[:], acc[:], rows[:, :, 0, 0:P], ALU.add))
            then_wait(nc.vector.tensor_tensor(acc[:], acc[:], ldb[:].unsqueeze(1).to_broadcast([P, NT, P]), ALU.add))
            dve.wait_ge(s_weight, 1)
            for n, (start, end) in enumerate(PIECES):
                dve.wait_ge(s_res[n], 16)
                for j in range(start, end):
                    last = nc.vector.scalar_tensor_tensor(acc[:, j, :], back[:, j, 0:P], weight[:, 0, j:j + 1],
                                                          acc[:, j, :], ALU.mult, ALU.add)
                if n == POOL_PIECE:
                    last.then_inc(s_first, 1)
                else:
                    then_wait(last)
                    dve.wait_ge(s_second, n + 1)
                    nc.vector.tensor_tensor(acc[:, start:end, :], acc[:, start:end, :], back[:, start:end, P:2 * P],
                                            ALU.add).then_inc(s_acc[n], 1)

        @block.tensor
        def _(pe):
            mm = nc.tensor.matmul

            def transpose_chunk(c):
                for i in range(TC):
                    j = c * TC + i
                    pe.wait_ge(s_xn[c], i + 1)
                    last = nc.tensor.transpose(ps[:, GATE[c], i * P:(i + 1) * P], rows[:, j, 0, 0:P], ident[:])
                last.then_inc(s_xnt_ps, 1)

            def logits_chunk(c):
                g = [n for n, (start, end) in enumerate(GROUPS) if start <= c * TC < end][0]
                start, end = GROUPS[g]
                if g >= 2:
                    pe.wait_ge(s_slot, g - 1)
                pe.wait_ge(s_xnt, c + 1)
                for j in range(c * TC, (c + 1) * TC):
                    last = mm(logit_ps[g][:, j - start, :], xn_t[:, j * P:(j + 1) * P], wgate[:], start=True, stop=True,
                              skip_group_check=True)
                if (c + 1) * TC == end:
                    last.then_inc(s_logits, 1)

            def projections(c):
                pe.wait_ge(s_xg, c + 1)
                for d in range(2):
                    if c:
                        pe.wait_ge(s_pj, 2 * (c - 1) + d + 1)
                    mm(bank(PROJ[d]), watt[:, W_X + d, :], xg_t[:, chunk(c)], start=True, stop=True).then_inc(s_pj_ps, 1)

            def gates(c, d):
                pe.wait_ge(s_pj, 2 * c + d + 1)
                for n, w in enumerate((W_GX, W_GA)):
                    if c:
                        pe.wait_ge(s_gate, 4 * (c - 1) + 2 * d + n + 1)
                    mm(bank(GATE[2 * d + n]), watt[:, w + d, :], proj[:, d, chunk(c)],
                       start=True, stop=True).then_inc(s_gate_ps, 1)

            def keep_warm(b, n):
                for _ in range(n):
                    mm(bank(b), ones[:], ones[:].unsqueeze(1).to_broadcast([P, 4, P]), start=True, stop=True)

            def ranks(g):
                pe.wait_ge(s_mask, g + 1)
                start, end = GROUPS[g]
                n = end - start
                mm(rank_ps[g], ones[0:1, :], slot_base[:, 0:n, :], start=True, stop=False)
                mm(rank_ps[g], before[:], mask[:, start:end, :], start=False, stop=False)
                for j in range(end - 1):
                    to = slice(max(j + 1 - start, 0), n)
                    last = mm(rank_ps[g][:, to, :], ones[:], mask[:, j:j + 1, :].to_broadcast([P, n - to.start, E]),
                              start=False, stop=(j == end - 2))
                last.then_inc(s_rank, 1)

            pe.wait_ge(s_cst, 6)
            keep_warm(PROJ[0], 8)
            transpose_chunk(0)
            pe.wait_ge(s_wgate, 16)
            logits_chunk(0)
            keep_warm(PROJ[0], 4)
            transpose_chunk(1)
            transpose_chunk(2)
            logits_chunk(1)
            transpose_chunk(3)
            keep_warm(PROJ[0], 2)
            ranks(0)
            keep_warm(PROJ[0], 2)
            logits_chunk(2)
            keep_warm(PROJ[0], 1)
            logits_chunk(3)
            keep_warm(PROJ[0], 1)
            pe.wait_ge(s_wts, 48)
            projections(0)
            projections(1)
            ranks(1)
            pe.wait_ge(s_xnt, NC)
            gates(0, 0)
            gates(0, 1)
            projections(2)
            gates(1, 0)
            gates(1, 1)
            ranks(2)
            projections(3)
            gates(2, 0)
            gates(2, 1)
            gates(3, 0)
            gates(3, 1)

            def twice_xn(c):
                mm(bank(OUT[c]), twice[:], xn_t[:, chunk(c)], start=True, stop=False)

            def outputs(c):
                pe.wait_ge(s_h, 2 * c + 1)
                mm(bank(OUT[c]), watt[:, W_O, :], gate_x[:, 0, chunk(c)], start=False, stop=False)
                pe.wait_ge(s_h, 2 * c + 2)
                mm(bank(OUT[c]), watt[:, W_O + 1, :], gate_x[:, 1, chunk(c)], start=False, stop=True).then_inc(s_o_ps, 1)

            def last_projection(c):
                pe.wait_ge(s_g, c + 1)
                for i in range(TC):
                    j = c * TC + i
                    last = mm(ps[:, LD[c], i * P:(i + 1) * P], xg_t[:, j * P:(j + 1) * P], watt[:, W_LD, :],
                              start=True, stop=True, skip_group_check=True)
                last.then_inc(s_ld_ps, 1)

            pe.wait_ge(s_cst, 7)
            pe.wait_ge(s_pj, 2 * NC)
            twice_xn(2)
            twice_xn(3)
            pe.wait_ge(s_gate, 4 * NC)
            twice_xn(0)
            twice_xn(1)
            keep_warm(LD[1], 2)
            outputs(0)
            outputs(1)
            last_projection(0)
            outputs(2)
            last_projection(1)
            outputs(3)

            pe.sem_inc(s_up, 4)
            pe.sem_inc(s_down, 2)

            def transpose_rows(it, r):
                pe.wait_ge(s_xe[r], it * 16 + 16)
                pe.wait_ge(s_xet, it * 2 + r + 1)
                for n in range(PT):
                    last = nc.tensor.transpose(xet_ps[:, n * P:(n + 1) * P], xe[:, r, n, 0:P], ident[:])
                last.then_inc(s_xet_ps, 1)

            def up(it, s):
                r, o = s // 2, s % 2
                if o == 0:
                    pe.wait_ge(s_xet, it * 2 + r + 2)
                    pe.wait_ge(s_w1[r], it * 16 + 16)
                pe.wait_ge(s_gelu, it * 4 + s + 1)
                for b in range(FB):
                    last = mm(ps[:, HID[o] + b, 0:CAP], w1[:, r, o, b * P:(b + 1) * P],
                              xe_t[:, r, o * CAP:(o + 1) * CAP], start=True, stop=True)
                last.then_inc(s_up, 1)

            def down(it, s):
                r, o = s // 2, s % 2
                if o == 0:
                    pe.wait_ge(s_w2[r], it * 16 + 16)
                pe.wait_ge(s_gelu, it * 4 + s + 3)
                pe.wait_ge(s_y, it * 4 + s + 1)
                for n in range(3):
                    for b in range(FB):
                        last = mm(ps[:, RES[o], n * P:(n + 1) * P], hid[:, o, b, n * P:(n + 1) * P],
                                  w2[:, r, o, b, :], start=(b == 0), stop=(b == FB - 1))
                last.then_inc(s_down, 1)

            pe.wait_ge(s_g, 2)
            transpose_rows(0, 0)
            pe.wait_ge(s_slot, len(GROUPS))
            last_projection(2)
            last_projection(3)
            pe.wait_ge(s_ld, 2)
            with pe.Fori(0, NP // 2 - 1) as it:
                up(it, 0)
                up(it, 1)
                transpose_rows(it, 1)
                down(it, 0)
                down(it, 1)
                up(it, 2)
                up(it, 3)
                transpose_rows(it + 1, 0)
                down(it, 2)
                down(it, 3)
            it = NP // 2 - 1
            up(it, 0)
            up(it, 1)
            transpose_rows(it, 1)
            down(it, 0)
            down(it, 1)
            up(it, 2)
            up(it, 3)
            down(it, 2)
            down(it, 3)


def kernel(**inputs):
    import numpy as np
    import concourse.bacc as bacc
    from concourse.bass_utils import run_bass_kernel_spmd

    fp32 = mybir.dt.float32
    a = {k: np.asarray(v) for k, v in inputs.items()}
    att = {k[len("L0_attn_"):]: v for k, v in a.items() if k.startswith("L0_attn_")}
    both = [f"{d}_{n}" for n in ("Wx", "Wgx", "Wga", "Wo") for d in ("fwd", "bwd")]
    cols = [f"{d}_{n}" for n in ("a_logit", "bx", "bgx", "bga", "bo") for d in ("fwd", "bwd")]
    x = att["x"]
    arrays = {
        "x_d": x.reshape(16, 128, 128).transpose(1, 0, 2).reshape(128, 2048),
        "w_att_d": np.concatenate([att[n] for n in both] + [att["ld_W"]], axis=1),
        "w_gate_d": a["L0_ffn_gate_w"].T,
        "cols_d": np.stack([att[n] for n in cols], axis=1),
        "ldb_d": att["ld_b"].reshape(128),
        "w1_d": a["L0_ffn_w1"],
        "w2_d": a["L0_ffn_w2"].reshape(16, 2, 128, 128).transpose(0, 2, 1, 3).reshape(16, 128, 256),
    }
    arrays = {k: np.ascontiguousarray(v) for k, v in arrays.items()}
    nc = bacc.Bacc("TRN2", target_bir_lowering=False, num_devices=1)
    aps = [nc.dram_tensor(k, v.shape, fp32, kind="ExternalInput").ap() for k, v in arrays.items()]
    out = nc.dram_tensor("out_d", (128, 2048), fp32, kind="ExternalOutput").ap()
    rglru_moe(nc, *aps, out)
    r = run_bass_kernel_spmd(nc, [arrays], core_ids=[0])
    y = r.results[0]["out_d"]
    return y.reshape(128, 16, 128).transpose(1, 0, 2).reshape(x.shape)
```
